# Optimizing a Trainium2 kernel written in Bass

```python
import numpy as np
import jax
import jax.numpy as jnp

def _softmax(x, axis=-1):
    return jax.nn.softmax(x, axis=axis)

def _gelu(x):
    return jax.nn.gelu(x, approximate=True)

def _silu(x):
    return jax.nn.silu(x)

def _sigmoid(x):
    return jax.nn.sigmoid(x)

def _layernorm(x, axis=-1, eps=1e-05):
    m = jnp.mean(x, axis=axis, keepdims=True)
    v = jnp.var(x, axis=axis, keepdims=True)
    return (x - m) / jnp.sqrt(v + eps)

def _scatter_add(tgt, idx, src, axis=0):
    return tgt.at[idx].add(src)

def _segment_sum(src, seg, n):
    return jax.ops.segment_sum(src, seg, n)
kernel_name = 'mk_cond_resid_d2_seqx_r2_b5b44a'

def setup_inputs(seed: int=0):
    np.random.seed(seed)
    _w = jnp.asarray

    def _rec_inputs():
        import jax
        import jax.numpy as jnp
        _rk = jax.random.key(seed)
        x = 7.22e-05 + 1 * jax.random.normal(jax.random.fold_in(_rk, 1), (8, 1024, 512), jnp.float32)
        _lenS = 1024 - jax.random.randint(jax.random.fold_in(_rk, 7), (8,), 0, max(1, 1024 // 4) + 1, jnp.int32)
        _lenS2 = 1024 - jax.random.randint(jax.random.fold_in(_rk, 8), (8,), 0, max(1, 1024 // 4) + 1, jnp.int32)
        cond_2048 = 0.997298 + 0.498944 * jax.random.normal(jax.random.fold_in(_rk, 11), (8, 1024), jnp.float32)
        return (x, cond_2048)
    x, cond_2048 = _rec_inputs()

    def _L0_cond_setup():
        import jax, jax.numpy as jnp
        import numpy as np
        EPS_IN = 1e-05
        EPS_DM = 1e-08

        def _dcoef(weight, style):
            return jax.lax.rsqrt(jnp.einsum('oi,bi->bo', jnp.square(weight), jnp.square(style)) + EPS_DM)
        key = jax.random.key(seed)
        ks = jax.random.split(key, 7)
        B, S, H = (8, 512, 512)
        lim = 1.0 / np.sqrt(H)
        u = lambda k, shp: jax.random.uniform(k, shp, jnp.float32, -lim, lim)
        return {'x': jax.random.normal(ks[0], (B, S, H), jnp.float32), 'q_weight': u(ks[1], (H, H)), 'k_weight': u(ks[2], (H, H)), 'v_weight': u(ks[3], (H, H)), 'w_weight': u(ks[4], (H, H)), 'u_weight': u(ks[5], (H, H)), 'styles': jax.random.normal(ks[6], (B, 2 * H), jnp.float32) * 0.5 + 1.0, 'num_heads': 16}
    _L0_cond_all = _L0_cond_setup()
    _L0_cond_in = {k: v for k, v in _L0_cond_all.items() if k in ('q_weight', 'k_weight', 'v_weight', 'w_weight', 'u_weight')}
    del _L0_cond_all

    def _L1_cond_setup():
        import jax, jax.numpy as jnp
        import numpy as np
        B, S, D_MODEL, D_INNER, D_STATE = (4, 2048, 512, 1024, 16)
        key = jax.random.key(seed)
        ks = jax.random.split(key, 12)
        inp = {'x': jax.random.normal(ks[0], (B, S, D_MODEL), jnp.float32), 't_emb': jax.random.normal(ks[1], (B, D_INNER), jnp.float32), 'W_in': jax.random.normal(ks[2], (2 * D_INNER, D_MODEL), jnp.float32) * 0.02, 'W_conv': jax.random.normal(ks[3], (D_INNER, 1, 4), jnp.float32) * 0.1, 'b_conv': jnp.zeros((D_INNER,), jnp.float32), 'ln_g': jnp.ones((D_INNER,), jnp.float32), 'ln_b': jnp.zeros((D_INNER,), jnp.float32), 'W_xproj': jax.random.normal(ks[4], (3 * D_STATE, D_INNER), jnp.float32) * 0.02, 'W_dt': jax.random.normal(ks[5], (D_STATE, D_STATE), jnp.float32) * 0.01, 'b_dt': jax.random.uniform(ks[6], (D_STATE,), jnp.float32) * 0.1, 'A_log': jax.random.normal(ks[7], (D_STATE,), jnp.float32) * 0.1, 'D': jnp.ones((D_INNER,), jnp.float32) * 0.1, 'W_out': jax.random.normal(ks[8], (D_MODEL, D_INNER), jnp.float32) * 0.02}
        return inp
    _L1_cond_all = _L1_cond_setup()
    _L1_cond_in = {k: v for k, v in _L1_cond_all.items() if k in ('W_in', 'W_conv', 'b_conv', 'ln_g', 'ln_b', 'W_xproj', 'W_dt', 'b_dt', 'A_log', 'D', 'W_out')}
    del _L1_cond_all
    return {'x': x, 'cond_2048': cond_2048, 'L0_cond_q_weight': _L0_cond_in['q_weight'], 'L0_cond_k_weight': _L0_cond_in['k_weight'], 'L0_cond_v_weight': _L0_cond_in['v_weight'], 'L0_cond_w_weight': _L0_cond_in['w_weight'], 'L0_cond_u_weight': _L0_cond_in['u_weight'], 'L1_cond_W_in': _L1_cond_in['W_in'], 'L1_cond_W_conv': _L1_cond_in['W_conv'], 'L1_cond_b_conv': _L1_cond_in['b_conv'], 'L1_cond_ln_g': _L1_cond_in['ln_g'], 'L1_cond_ln_b': _L1_cond_in['ln_b'], 'L1_cond_W_xproj': _L1_cond_in['W_xproj'], 'L1_cond_W_dt': _L1_cond_in['W_dt'], 'L1_cond_b_dt': _L1_cond_in['b_dt'], 'L1_cond_A_log': _L1_cond_in['A_log'], 'L1_cond_D': _L1_cond_in['D'], 'L1_cond_W_out': _L1_cond_in['W_out']}

def reference(x, cond_2048, L0_cond_q_weight, L0_cond_k_weight, L0_cond_v_weight, L0_cond_w_weight, L0_cond_u_weight, L1_cond_W_in, L1_cond_W_conv, L1_cond_b_conv, L1_cond_ln_g, L1_cond_ln_b, L1_cond_W_xproj, L1_cond_W_dt, L1_cond_b_dt, L1_cond_A_log, L1_cond_D, L1_cond_W_out):
    import jax
    import jax.numpy as jnp

    def _L0_cond_ref(x, q_weight, k_weight, v_weight, w_weight, u_weight, styles, num_heads):
        import jax, jax.numpy as jnp
        import numpy as np
        EPS_IN = 1e-05
        EPS_DM = 1e-08

        def _dcoef(weight, style):
            return jax.lax.rsqrt(jnp.einsum('oi,bi->bo', jnp.square(weight), jnp.square(style)) + EPS_DM)
        B, S, H = x.shape
        nh = num_heads
        d = H // nh
        scale = jnp.asarray(d, x.dtype) ** (-0.5)
        s1 = styles[:, :H]
        s2 = styles[:, H:]
        x = x * s1[:, None, :]
        mu = jnp.mean(x, axis=-1, keepdims=True)
        var = jnp.mean(jnp.square(x - mu), axis=-1, keepdims=True)
        x = (x - mu) * jax.lax.rsqrt(var + EPS_IN)
        q_dc = _dcoef(q_weight, s1)
        k_dc = _dcoef(k_weight, s1)
        v_dc = _dcoef(v_weight, s1)
        w_dc = _dcoef(w_weight, s2)
        u_dc = _dcoef(u_weight, s2)

        def heads(t):
            return t.reshape(B, S, nh, d).transpose(0, 2, 1, 3)
        q = heads(jnp.einsum('bsh,oh->bso', x, q_weight) * q_dc[:, None, :])
        k = heads(jnp.einsum('bsh,oh->bso', x, k_weight) * k_dc[:, None, :])
        v_flat = jnp.einsum('bsh,oh->bso', x, v_weight) * v_dc[:, None, :] * s2[:, None, :]
        skip = v_flat
        v = heads(v_flat)
        attn = jnp.einsum('bhqd,bhkd->bhqk', q, k) * scale
        attn = jax.nn.softmax(attn, axis=-1)
        out = jnp.einsum('bhqk,bhkd->bhqd', attn, v).transpose(0, 2, 1, 3).reshape(B, S, H)
        out = jnp.einsum('bsh,oh->bso', out, w_weight) * w_dc[:, None, :]
        skip = jnp.einsum('bsh,oh->bso', skip, u_weight) * u_dc[:, None, :]
        return out + skip

    def _L1_cond_ref(x, t_emb, W_in, W_conv, b_conv, ln_g, ln_b, W_xproj, W_dt, b_dt, A_log, D, W_out):
        import jax, jax.numpy as jnp
        import numpy as np
        B, S, D_MODEL, D_INNER, D_STATE = (4, 2048, 512, 1024, 16)
        d_inner = W_conv.shape[0]
        d_state = A_log.shape[0]
        xr, gate = jnp.split(x @ W_in.T, 2, axis=-1)
        xr = xr + t_emb[:, None, :]
        xc = jax.lax.conv_general_dilated(xr.transpose(0, 2, 1), W_conv, (1,), [(3, 0)], feature_group_count=d_inner, dimension_numbers=('NCH', 'OIH', 'NCH')) + b_conv[None, :, None]
        xc = jax.nn.silu(xc).transpose(0, 2, 1)
        mu = xc.mean(-1, keepdims=True)
        var = xc.var(-1, keepdims=True)
        xn = (xc - mu) / jnp.sqrt(var + 1e-05) * ln_g + ln_b
        Bm, Cm, dt = jnp.split(xn @ W_xproj.T, 3, axis=-1)
        dt = jnp.tanh(dt @ W_dt.T + b_dt) * 0.01
        A = -jnp.tanh(A_log)
        Ad = 1.0 + dt * A
        Bd = Bm * jnp.minimum(jnp.linalg.norm(xn, axis=-1, keepdims=True), 1.0)
        h0 = jnp.zeros((xn.shape[0], d_state, d_inner), xn.dtype)

        def step(h, inputs):
            ad, bd, xt, ct = inputs
            h = jnp.clip(h * ad[:, :, None] + bd[:, :, None] * xt[:, None, :], -10.0, 10.0)
            yt = jnp.einsum('bd,bdh->bh', ct, h)
            return (h, yt)
        _, ys = jax.lax.scan(step, h0, (Ad.transpose(1, 0, 2), Bd.transpose(1, 0, 2), xn.transpose(1, 0, 2), Cm.transpose(1, 0, 2)))
        y = ys.transpose(1, 0, 2) + D * xn
        return y * jax.nn.silu(gate) @ W_out.T
    x = x + _L0_cond_ref(x, L0_cond_q_weight, L0_cond_k_weight, L0_cond_v_weight, L0_cond_w_weight, L0_cond_u_weight, cond_2048, 16)
    x = x + _L1_cond_ref(x, cond_2048, L1_cond_W_in, L1_cond_W_conv, L1_cond_b_conv, L1_cond_ln_g, L1_cond_ln_b, L1_cond_W_xproj, L1_cond_W_dt, L1_cond_b_dt, L1_cond_A_log, L1_cond_D, L1_cond_W_out)
    return x

_drawn_inputs = setup_inputs


def setup_inputs(seed=0):
    import zlib

    import numpy as np

    out = dict(_drawn_inputs(seed))
    spreads = {'L1_cond_b_conv': (0.0, 0.1),
     'L1_cond_ln_g': (1.0, 0.2),
     'L1_cond_ln_b': (0.0, 0.1),
     'L1_cond_D': (0.10000000149011612, 0.6)}
    factors = {'L1_cond_W_dt': 8.0, 'L1_cond_b_dt': 8.0, 'L1_cond_A_log': 8.0}
    for name, (base, spread) in spreads.items():
        noise = np.random.default_rng([zlib.crc32(name.encode()), seed]).standard_normal(out[name].shape)
        drawn = base * np.exp(spread * noise) if base else spread * noise
        out[name] = jnp.asarray(drawn.astype(out[name].dtype))
    for name, factor in factors.items():
        out[name] = (out[name] * factor).astype(out[name].dtype)
    return out
```

```python
from contextlib import ExitStack

import numpy as np

import concourse.bass as bass
from concourse import mybir

F32 = mybir.dt.float32
F32R = mybir.dt.float32r
ACT = mybir.ActivationFunctionType
ALU = mybir.AluOpType
AX = mybir.AxisListType

P = 128
HID = 512
HEADS = 16
DH = HID // HEADS
GH = P // DH
GROUPS = HEADS // GH
HT = HID // P
DIN = 1024
CT = DIN // P
NST = 16
EPS_LN = 1e-5
EPS_DEMOD = 1e-8
BANK = 512


class Queues:

    def __init__(self, nc, ctx):
        self.nc, self.ctx = nc, ctx
        self.q = {e: [] for e in ("pe", "act", "dve", "pool", "sp")}
        self.sems, self.count = {}, {}
        self.waited = {e: {} for e in self.q}

    def put(self, engine, make, after=(), signal=None, dma=False):
        for token in after:
            for tk in token if isinstance(token, list) else [token]:
                self.wait(engine, tk)
        if signal is None:
            self.q[engine].append(make)
            return None
        if signal not in self.sems:
            self.sems[signal] = self.ctx.enter_context(self.nc.semaphore(signal))
            self.count[signal] = 0
        sem, by = self.sems[signal], 16 if dma else 1
        self.count[signal] += by
        self.q[engine].append(lambda e: make(e).then_inc(sem, by))
        return signal, self.count[signal]

    def wait(self, engine, token):
        if token is None:
            return
        name, value = token
        if self.waited[engine].get(name, 0) >= value:
            return
        self.waited[engine][name] = value
        sem = self.sems[name]
        self.q[engine].append(lambda e: e.wait_ge(sem, value))

    def dma(self, out, in_, after=(), signal=None, engine="sp"):
        out, in_ = (a.bitcast(F32) if a.dtype == F32R else a for a in (out, in_))
        return self.put(engine, lambda e: e.dma_start(out, in_), after, signal, dma=True)

    def emit(self):
        with self.nc.Block() as block:
            for name, reg in (("pe", block.tensor), ("act", block.scalar), ("dve", block.vector),
                              ("pool", block.gpsimd), ("sp", block.sync)):
                def body(e, name=name):
                    for f in self.q[name]:
                        f(e)
                reg(body)


class Background:

    def __init__(self):
        self.todo = []

    def add(self, gen):
        self.todo.append(gen)

    def advance(self, n):
        while n > 0 and self.todo:
            try:
                next(self.todo[0])
                n -= 1
            except StopIteration:
                self.todo.pop(0)

    def finish(self):
        while self.todo:
            self.advance(1)


def barrier(Q, name):
    tokens = []
    for e in ("pe", "act", "dve", "pool", "sp"):
        tokens.append(Q.put(e, lambda en: en.nop(), signal=f"{name}_{e}"))
    for e in Q.q:
        for t in tokens:
            Q.wait(e, t)


def attention_part(nc, Q, t, d, dims):
    B, S = dims["B"], dims["S"]
    TT = S // P
    QC = min(BANK, S)
    NQ = S // QC
    SCALE = float(DH) ** -0.5
    stack = ExitStack()
    sb = lambda n, s, dt=F32: stack.enter_context(nc.sbuf_tensor(n, s, dt))
    pb = lambda n, s, dt=F32: stack.enter_context(nc.psum_tensor(n, s, dt))

    ident, ones32 = t["ident"], t["ones32"]
    wv = sb("wv", [P, HT, HID])
    qk_dc = sb("qk_dc", [P, 2, HT, B])
    rstd = sb("rstd", [P, B * TT])
    nmr = sb("nmr", [P, B * TT])
    misc = [pb(f"misc{i}", [P, BANK]) for i in range(2)]
    misc_free = [None, None]
    turn = [0]

    def take_misc():
        i = turn[0] % 2
        turn[0] += 1
        return i

    setup = ExitStack()
    sbs = lambda n, s, dt=F32: setup.enter_context(nc.sbuf_tensor(n, s, dt))
    wsq = sbs("wsq", [P, 5, HT, HID])
    condT = sbs("condT_sb", [P, 2 * HT, B])
    s2row = sbs("s2row", [B, HID])
    rows = sbs("rows", [B, 3, HID])
    s1b = sbs("s1b", [P, 2, HID])
    xin = sbs("xin_s", [P, 4, HID])
    xms = sbs("xm_s", [P, 2, HID])
    bst = sbs("bst", [P, 2, 6])
    mv = sbs("mv", [P, B * TT, 2])

    cond_in = Q.dma(condT[:, :, :], d["condT"].rearrange("(t p) b -> p t b", p=P), signal="ld_cond")
    s2_in = Q.dma(s2row[:, :], d["cond"][:, HID:2 * HID], signal="ld_s2")
    w_in = [Q.dma(wsq[:, n, :, :], d[w].rearrange("(t p) o -> p t o", p=P), signal=f"ld_w{n}")
            for n, w in enumerate(("wqT", "wkT", "wvT", "wwT", "wuT"))]
    wv_in = Q.dma(wv[:, :, :], d["wvT"].rearrange("(t p) o -> p t o", p=P), signal="ld_wv")
    cond_sq = Q.put("act", lambda e: e.activation(condT[:, :, :], condT[:, :, :], ACT.Square),
                    [cond_in], "setup_act")
    sq = [Q.put("act", lambda e, n=n: e.activation(wsq[:, n, :, :], wsq[:, n, :, :], ACT.Square),
                [w_in[n]], "setup_act") for n in range(5)]
    m = take_misc()
    for n in range(2):
        for ot in range(HT):
            for it in range(HT):
                last = (n == 1 and ot == HT - 1 and it == HT - 1)
                c = (n * HT + ot) * B
                tok = Q.put("pe", lambda e, n=n, ot=ot, it=it, c=c: e.matmul(
                    misc[0][:, c:c + B], wsq[:, n, it, ot * P:(ot + 1) * P], condT[:, it, :],
                    start=it == 0, stop=it == HT - 1), [cond_sq, sq[n]], "setup_pe" if last else None)
    flat = qk_dc[:, :, :, :].rearrange("p n o b -> p (n o b)")
    tok = Q.put("dve", lambda e: e.tensor_scalar(flat, misc[0][:, 0:2 * HT * B], EPS_DEMOD, None, ALU.add),
                [tok], "setup_dve")
    qk_free = tok
    tok = Q.put("act", lambda e: e.activation(flat, flat, ACT.Sqrt), [tok], "setup_act")
    qk_ready = Q.put("dve", lambda e: e.reciprocal(flat, flat), [tok], "setup_dve")
    bank_free = [qk_free, None]
    row_tok = None
    for j, n in enumerate((2, 3, 4)):
        m = (j + 1) % 2
        h0 = 0 if n == 2 else HT
        for it in range(HT):
            tok = Q.put("pe", lambda e, n=n, it=it, m=m, h0=h0: e.matmul(
                misc[m][0:B, :], condT[:, h0 + it, :], wsq[:, n, it, :], start=it == 0, stop=it == HT - 1),
                [sq[n], bank_free[m]], "setup_pe" if it == HT - 1 else None)
        tok = Q.put("dve", lambda e, j=j, m=m: e.tensor_scalar(rows[:, j, :], misc[m][0:B, :], EPS_DEMOD, None,
                                                               ALU.add), [tok], "setup_dve")
        bank_free[m] = tok
        row_tok = Q.put("act", lambda e, j=j: e.activation(rows[:, j, :], rows[:, j, :], ACT.Sqrt),
                        [tok], "setup_act")
    tok = Q.put("dve", lambda e: e.reciprocal(rows[:, :, :], rows[:, :, :]), [row_tok], "setup_dve")
    tok = Q.put("dve", lambda e: e.tensor_tensor(rows[:, 0, :], rows[:, 0, :], s2row[:, :], ALU.mult),
                [tok, s2_in], "setup_dve")
    rows_out = Q.dma(d["rows"], rows[:, :, :], [tok], "st_rows")
    s1_free, x_free, xm_free = [None] * 2, [None] * 4, [None] * 2
    st_tok = None
    for b in range(B):
        s1_in = Q.dma(s1b[:, b % 2, :], d["cond"][b, 0:HID].partition_broadcast(P), [s1_free[b % 2]],
                      f"ld_s1_{b % 2}")
        for tt in range(TT):
            i = b * TT + tt
            x_in = Q.dma(xin[:, i % 4, :], d["x"][b, tt * P:(tt + 1) * P, :], [x_free[i % 4]], f"ld_xs{i % 4}")
            mul = Q.put("pool", lambda e, i=i, b=b: e.tensor_tensor(
                xms[:, i % 2, :], xin[:, i % 4, :], s1b[:, b % 2, :], ALU.mult),
                [x_in, s1_in, xm_free[i % 2]], "stat_pool")
            x_free[i % 4] = s1_free[b % 2] = mul
            tok = Q.put("dve", lambda e, i=i: e.bn_stats(bst[:, i % 2, :], xms[:, i % 2, :]), [mul], "stat_dve")
            xm_free[i % 2] = tok
            st_tok = Q.put("dve", lambda e, i=i: e.bn_aggr(mv[:, i, :], bst[:, i % 2, :]), [tok], "stat_dve")
    tok = Q.put("dve", lambda e: e.tensor_scalar(rstd[:, :], mv[:, :, 1], EPS_LN, None, ALU.add),
                [st_tok], "stat_dve")
    tok = Q.put("act", lambda e: e.activation(rstd[:, :], rstd[:, :], ACT.Sqrt), [tok], "stat_act")
    tok = Q.put("dve", lambda e: e.reciprocal(rstd[:, :], rstd[:, :]), [tok], "stat_dve")
    stats_ready = Q.put("dve", lambda e: e.scalar_tensor_tensor(
        nmr[:, :], mv[:, :, 0], -1.0, rstd[:, :], ALU.mult, ALU.mult), [tok], "stat_dve")
    for e in ("pe", "act", "dve", "pool", "sp"):
        for tk in (stats_ready, qk_ready, rows_out, wv_in):
            Q.wait(e, tk)
    barrier(Q, "b0")
    setup.close()

    wqk = sb("wqk", [P, 2, 2, HT, P])
    wwu = sb("wwu", [P, 2, HT, HID])
    xhT = sb("xhT", [P, HT, S])
    V = sb("V", [P, 2, TT, HID])
    qhat = sb("qhat", [P, 2, GH, S], F32R)
    khat = sb("khat", [P, 2, GH, S], F32R)
    halves = sb("halves", [P, 2, 2, QC], F32R)
    prob = sb("prob", [P, 2 * GH, QC])
    aoT = sb("aoT", [P, GROUPS, S])
    xt = sb("xt", [P, 2, HID])
    xh = sb("xh", [P, HID])
    vTt = sb("vTt", [P, HT, P])
    brow = sb("brow", [P, 4, HID])
    mx2 = sb("mx2", [P, GH * TT, NQ])
    mx = sb("mx", [P, GH * TT])
    mrow = sb("mrow", [GH * TT, 2, P], F32R)
    rsum = sb("rsum", [P, QC])
    smax = [pb(f"smax{i}", [P, BANK]) for i in range(2)]
    sexp = [pb(f"sexp{i}", [P, BANK]) for i in range(2)]
    av = pb("av", [P, BANK])
    sums = pb("sums", [P, BANK])

    ones_tok = None
    for i in range(2):
        ones_tok = Q.put("dve", lambda e, i=i: e.memset(khat[96:98, i, :, :].bitcast(F32), 1.0), signal="kones")

    smax_free, sexp_free = [None] * 2, [None] * 2
    prob_free = [None] * (2 * GH)
    prob_done = [None] * (2 * GH)
    hat_free = [None, None]
    hat_tok = [None, None]
    mrow_tok = [None, None]
    halves_free = [None] * 4
    xhT_free, xhT_ready = [None], [None]
    V_free, V_ready = [None, None], [None, None]
    brow_tok, brow_free = [None], [None]
    wwu_ready, wwu_free, wwu_scaled = [None], [None], [None]
    aoT_free = [None] * 1
    aoT_ready = {}
    xt_free = [None, None]
    xh_free, vTt_free = [None], [None]
    wqk_tok = {}
    wqk_free = [None, None]
    xt_turn = [0]

    def load_group_weights(u):
        g, s = u % GROUPS, u % 2
        toks = [Q.dma(wqk[:, s, n, :, :], d[w][:, g * P:(g + 1) * P].rearrange("(t p) o -> p t o", p=P),
                      [wqk_free[s]], f"ld_wqk{s}{n}") for n, w in enumerate(("wqT", "wkT"))]
        wqk_tok[s] = toks

    def start_batch(b):
        after = [brow_free[0]]
        Q.dma(brow[:, 0, :], d["cond"][b, 0:HID].partition_broadcast(P), after, "ld_brow")
        brow_tok[0] = Q.dma(brow[:, 1, :], d["rows"][b, 0].partition_broadcast(P), (), "ld_brow")
        xts = {}

        def load_x(tt):
            s = xt_turn[0] % 2
            xt_turn[0] += 1
            xts[tt] = (s, Q.dma(xt[:, s, :], d["x"][b, tt * P:(tt + 1) * P, :], [xt_free[s]], f"ld_xt{s}"))
        load_x(0)
        for tt in range(TT):
            if tt + 1 < TT:
                load_x(tt + 1)
            s, x_in = xts[tt]
            i = b * TT + tt
            mod = Q.put("pool", lambda e, s=s: e.tensor_tensor(xt[:, s, :], xt[:, s, :], brow[:, 0, :], ALU.mult),
                        [x_in, brow_tok[0]], "ln_pool")
            nrm = Q.put("act", lambda e, s=s, i=i: e.activation(
                xh[:, :], xt[:, s, :], ACT.Identity, bias=nmr[:, i:i + 1], scale=rstd[:, i:i + 1]),
                [mod, xh_free[0]], "ln_act")
            xt_free[s] = nrm
            m = take_misc()
            for it in range(HT):
                tr = Q.put("pe", lambda e, it=it, m=m: e.transpose(
                    misc[m][:, it * P:(it + 1) * P], xh[:, it * P:(it + 1) * P], ident[:, :]),
                    [nrm, misc_free[m]], "ln_pe" if it == HT - 1 else None)
            xh_free[0] = tr
            cp = Q.put("act", lambda e, m=m, tt=tt: e.activation(
                xhT[:, :, tt * P:(tt + 1) * P], misc[m][:, :].rearrange("p (t q) -> p t q", t=HT), ACT.Copy),
                [tr, xhT_free[0]], "ln_act")
            misc_free[m] = cp
            xhT_ready[0] = cp
            yield
            m = take_misc()
            for it in range(HT):
                mm = Q.put("pe", lambda e, it=it, m=m, tt=tt: e.matmul(
                    misc[m][:, :], xhT[:, it, tt * P:(tt + 1) * P], wv[:, it, :], start=it == 0, stop=it == HT - 1),
                    [cp, misc_free[m]], "v_pe" if it == HT - 1 else None)
            vt = Q.put("dve", lambda e, m=m, tt=tt, b=b: e.tensor_tensor(
                V[:, b % 2, tt, :], misc[m][:, :], brow[:, 1, :], ALU.mult), [mm, V_free[b % 2]], "v_dve")
            misc_free[m] = vt
            V_ready[b % 2] = vt
            yield
        brow_free[0] = vt

    def scale_output_weights(b):
        r_tok = Q.dma(brow[:, 2:4, :], d["rows"][b, 1:3].rearrange("n h -> (n h)").partition_broadcast(P)
                      .rearrange("p (n h) -> p n h", n=2), [wwu_scaled[0]], "ld_wurow")
        for n, w in enumerate(("wwT", "wuT")):
            w_tok = Q.dma(wwu[:, n, :, :], d[w].rearrange("(t p) o -> p t o", p=P), [wwu_free[0]], "ld_wwu")
        for n in range(2):
            for ot in range(HT):
                sc = Q.put("pool", lambda e, n=n, ot=ot: e.tensor_tensor(
                    wwu[:, n, ot, :], wwu[:, n, ot, :], brow[:, 2 + n, :], ALU.mult), [w_tok, r_tok], "wu_pool")
                yield
        wwu_scaled[0] = wwu_ready[0] = sc

    def start_group(u):
        b, g, s = u // GROUPS, u % GROUPS, u % 2
        w_tok = wqk_tok[s]
        for c in range(NQ):
            for n in range(2):
                m = take_misc()
                for it in range(HT):
                    mm = Q.put("pe", lambda e, it=it, m=m, n=n, c=c: e.matmul(
                        misc[m][:, 0:QC], wqk[:, s, n, it, :], xhT[:, it, c * QC:(c + 1) * QC],
                        start=it == 0, stop=it == HT - 1),
                        [xhT_ready[0], w_tok[n], misc_free[m]], "qk_pe" if it == HT - 1 else None)
                dc = qk_dc[:, n, g, b:b + 1]
                hi = Q.put("act", lambda e, m=m, n=n, dc=dc: e.activation(
                    halves[:, n, 0, :], misc[m][:, 0:QC], ACT.Copy, scale=dc), [mm, halves_free[2 * n]], "qk_act")
                lo = Q.put("dve", lambda e, m=m, n=n, dc=dc: e.scalar_tensor_tensor(
                    halves[:, n, 1, :], misc[m][:, 0:QC], dc, halves[:, n, 0, :].bitcast(F32), ALU.mult,
                    ALU.subtract), [hi, halves_free[2 * n + 1]], "qk_dve")
                misc_free[m] = lo
                hat = (qhat, khat)[n]
                for h in range(GH):
                    for r, half in enumerate(((0, 1, 0), (0, 0, 1))[n]):
                        tk = Q.dma(hat[r * DH:(r + 1) * DH, s, h, c * QC:(c + 1) * QC],
                                   halves[h * DH:(h + 1) * DH, n, half, :],
                                   [(hi, lo)[half], hat_free[s]], f"hat{s}{n}{c % 2}")
                halves_free[2 * n] = halves_free[2 * n + 1] = tk
                hat_tok[s] = (hat_tok[s] or [])[-3:] + [tk]
                yield
        xhT_free[0] = mm
        wqk_free[s] = mm
        if u + 2 < B * GROUPS:
            load_group_weights(u + 2)
        toks = list(hat_tok[s])
        for h in range(GH):
            for qt in range(TT):
                for c in range(NQ):
                    m = c % 2
                    mm = Q.put("pe", lambda e, h=h, qt=qt, c=c, m=m: e.matmul(
                        smax[m][:, 0:QC], qhat[0:96, s, h, qt * P:(qt + 1) * P],
                        khat[0:96, s, h, c * QC:(c + 1) * QC], start=True, stop=True),
                        toks + [smax_free[m]], "smax_pe")
                    smax_free[m] = rd = Q.put("dve", lambda e, h=h, qt=qt, c=c, m=m: e.tensor_reduce(
                        mx2[:, h * TT + qt, c:c + 1], smax[m][:, 0:QC], AX.X, ALU.max), [mm], "smax_dve")
                yield
        rd = Q.put("dve", lambda e: e.tensor_reduce(mx[:, :], mx2[:, :, :], AX.X, ALU.max), [rd], "smax_dve")
        m = take_misc()
        n_rows = GH * TT
        tr = Q.put("pe", lambda e, m=m: e.transpose(misc[m][0:n_rows, 0:P], mx[:, :], ident[:, :]),
                   [rd, misc_free[m]], "mrow_pe")
        hi = Q.put("act", lambda e, m=m: e.activation(mrow[:, 0, :], misc[m][0:n_rows, 0:P], ACT.Copy, scale=-1.0),
                   [tr, mrow_tok[1 - s], mrow_tok[s]], "mrow_act")
        lo = Q.put("dve", lambda e, m=m: e.scalar_tensor_tensor(
            mrow[:, 1, :], misc[m][0:n_rows, 0:P], -1.0, mrow[:, 0, :].bitcast(F32), ALU.mult, ALU.subtract),
            [hi], "mrow_dve")
        misc_free[m] = lo
        for r in range(2):
            mrow_tok[s] = Q.dma(qhat[96 + r:97 + r, s, :, :].rearrange("p h (t q) -> p (h t) q", q=P),
                                mrow[:, r, :], [(hi, lo)[r], hat_free[s]], f"mrow{s}")
        yield

    def finish_batch(b):
        for tt in range(TT):
            s = xt_turn[0] % 2
            xt_turn[0] += 1
            x_in = Q.dma(xt[:, s, :], d["x"][b, tt * P:(tt + 1) * P, :], [xt_free[s]], f"ld_xt{s}")
            m = take_misc()
            for ot in range(HT):
                tr = Q.put("pe", lambda e, ot=ot, m=m, tt=tt: e.transpose(
                    misc[m][:, ot * P:(ot + 1) * P], V[:, b % 2, tt, ot * P:(ot + 1) * P], ident[:, :]),
                    [V_ready[b % 2], misc_free[m]], "fin_pe" if ot == HT - 1 else None)
            cp = Q.put("act", lambda e, m=m: e.activation(
                vTt[:, :, :], misc[m][:, :].rearrange("p (t q) -> p t q", t=HT), ACT.Copy),
                [tr, vTt_free[0]], "fin_act")
            misc_free[m] = cp
            yield
            m = take_misc()
            for ot in range(HT):
                Q.put("pe", lambda e, ot=ot, m=m, tt=tt: e.matmul(
                    misc[m][:, :], aoT[:, ot, tt * P:(tt + 1) * P], wwu[:, 0, ot, :], start=ot == 0, stop=False),
                    [aoT_ready[b], wwu_ready[0], misc_free[m]])
            for ot in range(HT):
                mm = Q.put("pe", lambda e, ot=ot, m=m: e.matmul(
                    misc[m][:, :], vTt[:, ot, :], wwu[:, 1, ot, :], start=False, stop=ot == HT - 1),
                    [cp], "fin_pe" if ot == HT - 1 else None)
            vTt_free[0] = mm
            add = Q.put("dve", lambda e, m=m, s=s: e.tensor_tensor(
                xt[:, s, :], misc[m][:, :], xt[:, s, :], ALU.add), [mm, x_in], "fin_dve")
            misc_free[m] = add
            x2_st = Q.dma(d["x2"][b, tt * P:(tt + 1) * P, :], xt[:, s, :], [add], f"st_x2_{s}")
            m = take_misc()
            for it in range(HT):
                tr = Q.put("pe", lambda e, it=it, m=m, s=s: e.transpose(
                    misc[m][:, it * P:(it + 1) * P], xt[:, s, it * P:(it + 1) * P], ident[:, :]),
                    [add, misc_free[m]], "fin_pe" if it == HT - 1 else None)
            cp = Q.put("act", lambda e, m=m: e.activation(xh[:, :], misc[m][:, :], ACT.Copy),
                       [tr, xh_free[0]], "fin_act")
            misc_free[m] = cp
            st = Q.dma(d["x2T"][:, b, tt * P:(tt + 1) * P].rearrange("(t p) q -> p t q", p=P),
                       xh[:, :].rearrange("p (t q) -> p t q", t=HT), [cp], "st_x2T")
            xh_free[0] = st
            xt_free[s] = [x2_st, tr]
            yield
        V_free[b % 2] = mm
        wwu_free[0] = mm
        aoT_free[0] = mm

    def attend(u, bg, rates):
        b, g, s = u // GROUPS, u % GROUPS, u % 2
        need = list(hat_tok[s]) + [mrow_tok[s], ones_tok]
        steps = [(c, kt) for c in range(NQ) for kt in range(TT)]
        state = {"av_free": attend.av_free, "scores": None}

        def score(n, h):
            c, kt = steps[n]
            bank, slot = (n * GH + h) % 2, (n % 2) * GH + h
            mm = Q.put("pe", lambda e: e.matmul(
                sexp[bank][:, 0:QC], khat[0:98, s, h, kt * P:(kt + 1) * P],
                qhat[0:98, s, h, c * QC:(c + 1) * QC], start=True, stop=True),
                need + [sexp_free[bank]], "sexp_pe")
            state["scores"] = mm
            prob_done[slot] = sexp_free[bank] = Q.put("act", lambda e: e.activation(
                prob[:, slot, :], sexp[bank][:, 0:QC], ACT.Exp, scale=SCALE), [mm, prob_free[slot]], "exp_act")

        def contract(n, which):
            c, kt = steps[n]
            for h in range(GH):
                slot = (n % 2) * GH + h
                out = (av, sums)[which]
                lhs = V[:, b % 2, kt, (g * GH + h) * DH:(g * GH + h + 1) * DH] if which == 0 else ones32[:, :]
                tok = Q.put("pe", lambda e, h=h, slot=slot, out=out, lhs=lhs: e.matmul(
                    out[h * DH:(h + 1) * DH, 0:QC], lhs, prob[:, slot, :], start=kt == 0, stop=kt == TT - 1),
                    [prob_done[slot], V_ready[b % 2], state["av_free"]], "av_pe" if h == GH - 1 else None)
            if which == 1:
                for h in range(GH):
                    prob_free[(n % 2) * GH + h] = tok
            if which == 1 and kt == TT - 1:
                rc = Q.put("dve", lambda e: e.reciprocal(rsum[:, :], sums[:, 0:QC]), [tok], "norm_dve")
                ao = Q.put("dve", lambda e: e.tensor_tensor(
                    aoT[:, g, c * QC:(c + 1) * QC], av[:, 0:QC], rsum[:, :], ALU.mult),
                    [rc, aoT_free[0]], "norm_dve")
                state["av_free"] = ao
                aoT_ready[b] = ao

        for n in range(len(steps) + 1):
            if n == len(steps) // 2:
                bg[0].finish()
            if n < len(steps):
                score(n, 0)
                score(n, 1)
            if n > 0:
                contract(n - 1, 0)
            if n < len(steps):
                score(n, 2)
            if n > 0:
                contract(n - 1, 1)
            if n < len(steps):
                score(n, 3)
            first = n < len(steps) // 2
            bg[0 if first else 1].advance(rates[0 if first else 1])
            if first:
                bg[1].advance(rates[2])
        hat_free[s] = state["scores"]
        attend.av_free = state["av_free"]
        bg[0].finish()
        bg[1].finish()
    attend.av_free = None

    U = B * GROUPS
    load_group_weights(0)
    if U > 1:
        load_group_weights(1)
    pre = Background()
    pre.add(start_batch(0))
    pre.add(start_group(0))
    pre.add(scale_output_weights(0))
    pre.finish()
    for u in range(U):
        b, g = divmod(u, GROUPS)
        bg = (Background(), Background())
        if g == 0 and b > 0:
            bg[0].add(finish_batch(b - 1))
            bg[0].add(scale_output_weights(b))
        n = 0
        if u + 1 < U:
            if (u + 1) % GROUPS == 0:
                bg[1].add(start_batch(b + 1))
                n += 2 * TT
            bg[1].add(start_group(u + 1))
            n += 2 * NQ + GH * TT + 1
        steps = NQ * TT
        if g == 0 and b > 0:
            rates = (-(-(2 * TT + 8) // (steps // 2)), -(-n // (steps // 2)), 1)
        else:
            rates = (0, -(-n // steps), -(-n // steps))
        attend(u, bg, rates)
    tail = Background()
    tail.add(finish_batch(B - 1))
    tail.finish()
    for name in ("st_x2_0", "st_x2_1", "st_x2T"):
        Q.wait("sp", (name, Q.count[name]))
    barrier(Q, "b1")
    stack.close()


def scan_part(nc, Q, t, d, dims):
    B, S = dims["B"], dims["S"]
    TOK = P
    NCH = S // TOK
    HB = B // 2
    UNIT = 8
    TAPS = 4
    NX = 3 * NST
    HC = TOK // 2
    ctx = ExitStack()
    sb = lambda n, s, dt=F32: ctx.enter_context(nc.sbuf_tensor(n, s, dt))
    pb = lambda n, s, dt=F32: ctx.enter_context(nc.psum_tensor(n, s, dt))
    ident = t["ident"]

    w_in = sb("w_in", [P, HT, 2 * DIN])
    w_out = sb("w_out", [P, CT, HID])
    wx = sb("wx", [P, CT, NX])
    affine = sb("affine", [P, 3, DIN])
    gw = sb("gw", [P, NX])
    bw = sb("bw", [P, NX])
    cols = sb("cols", [P, 3, CT])
    wconv = sb("wconv", [P, CT, TAPS])
    temb = sb("temb", [P, CT, B])
    state_cols = sb("state_cols", [P, 2])
    a_neg = sb("a_neg", [P, 1])
    spread = sb("spread", [P, P], F32R)
    mask = sb("mask", [P, 8, 32])
    halo = sb("halo", [P, CT, B, TAPS - 1])
    zeros = sb("zeros", [P, TOK])
    x2T = sb("x2T_sb", [P, HT, HB, TOK])
    xr = sb("xr", [P, 2, HB, TAPS - 1 + TOK])
    cv = sb("cv", [P, 2, HB, TOK])
    xc = sb("xc", [P, CT, HB, TOK])
    st6 = sb("st6", [P, 2, 2, 6])
    mvb = sb("mvb", [P, HB, 2])
    rs = sb("rs", [P, HB])
    nm = sb("nm", [P, HB])
    nmr = sb("nmr_b", [P, HB])
    xn = sb("xn", [P, 2, DIN])
    xhi = sb("xhi", [P, DIN], F32R)
    dx = sb("dx", [P, DIN])
    sumsq = sb("sumsq", [P, HB])
    proj = sb("proj", [P, HB, NX])
    projT = sb("projT", [NX, HB, TOK])
    par = sb("par", [P, 3, TOK])
    decay = sb("decay", [P, 2, TOK])
    inv = sb("inv", [P, TOK])
    bd = sb("bd", [P, 2, TOK])
    lim = sb("lim", [P, 2, 2, TOK])
    cd = sb("cd", [P, 2, TOK])
    cexp = sb("cexp", [P, 2, HC, 32])
    sx = sb("sx", [P, 3, UNIT // 4, DIN], F32R)
    g = sb("g", [P, 4, DIN])
    ysb = sb("ysb", [P, 2, BANK])
    y_t = sb("y_t", [P, DIN])
    dx_t = sb("dx_t", [P, DIN])
    sg = sb("sg", [P, DIN])
    ygT = sb("ygT", [P, CT, P])
    x2_t = sb("x2_t", [P, HID])
    x2T_t = sb("x2T_t", [P, HT, P])
    xps = [pb(f"xps{i}", [P, DIN]) for i in range(2)]
    yps = [pb(f"yps{i}", [P, BANK]) for i in range(2)]
    misc = [pb(f"miscb{i}", [P, BANK]) for i in range(2)]
    misc_free = [None, None]
    PREP, FIN = 0, 1

    ld = lambda out, in_, name: Q.dma(out, in_, (), name)
    w_in_tok = ld(w_in[:, :, :], d["w_inT"].rearrange("(t p) o -> p t o", p=P), "ldb_win")
    w_out_tok = ld(w_out[:, :, :], d["w_outT"].rearrange("(t p) o -> p t o", p=P), "ldb_wout")
    wx_tok = ld(wx[:, :, 0:2 * NST], d["wxT"].rearrange("(t p) o -> p t o", p=P)[:, :, 0:2 * NST], "ldb_wx")
    aff_tok = [ld(affine[:, n, :], d[k].partition_broadcast(P), f"ldb_a{n}") for n, k in
               enumerate(("ln_g", "ln_b", "D"))]
    cols_tok = [ld(cols[:, n, :], d[k], f"ldb_c{n}") for n, k in
                enumerate(("ln_g_cols", "ln_b_cols", "b_conv_cols"))]
    wconv_tok = ld(wconv[:, :, :], d["w_conv"].rearrange("(t p) k -> p t k", p=P), "ldb_wc")
    temb_tok = ld(temb[:, :, :], d["condT"].rearrange("(t p) b -> p t b", p=P), "ldb_te")
    sc_tok = ld(state_cols[:, :], d["state_cols"], "ldb_sc")
    mask_tok = ld(mask[:, :, :], d["mask"].rearrange("p (a m) -> p a m", a=8), "ldb_mask")
    spread_tok = ld(xn[:, 0, 0:P], d["spread"], "ldb_spread")
    wxdt_tok = ld(xn[0:NST, 1, :], d["wx"][2 * NST:NX, :], "ldb_wxdt")
    wdt_tok = ld(dx[0:NST, 0:NST], d["w_dtT"], "ldb_wdt")
    tok = Q.put("dve", lambda e: e.tensor_copy(spread[:, :], xn[:, 0, 0:P]), [spread_tok], "setb_dve")
    for ap in (halo[:, :, :, :], zeros[:, :], g[:, 3, :]):
        tok = Q.put("dve", lambda e, ap=ap: e.memset(ap, 0.0), (), "setb_dve")
    ones_tok = Q.put("dve", lambda e: e.memset(sg[:, 0:P], 1.0), (), "setb_dve")
    for ct in range(CT):
        tok = Q.put("pe", lambda e, ct=ct: e.matmul(
            misc[0][:, ct * NST:(ct + 1) * NST], xn[0:NST, 1, ct * P:(ct + 1) * P], dx[0:NST, 0:NST],
            start=True, stop=True), [wxdt_tok, wdt_tok], "setb_pe" if ct == CT - 1 else None)
    tok = Q.put("act", lambda e: e.activation(
        wx[:, :, 2 * NST:NX], misc[0][:, 0:CT * NST].rearrange("p (t k) -> p t k", t=CT), ACT.Copy),
        [tok], "setb_act")
    misc_free[0] = tok
    tmp = ygT
    for ct in range(CT):
        tok = Q.put("dve", lambda e, ct=ct: e.tensor_scalar(
            tmp[:, ct, 0:NX], wx[:, ct, :], cols[:, 1, ct:ct + 1], None, ALU.mult),
            [tok, wx_tok, cols_tok[1], cols_tok[0]], "setb_dve")
    for ct in range(CT):
        tok = Q.put("dve", lambda e, ct=ct: e.tensor_scalar(
            wx[:, ct, :], wx[:, ct, :], cols[:, 0, ct:ct + 1], None, ALU.mult), [tok], "setb_dve")
    for n, (src, dst) in enumerate(((wx, gw), (tmp, bw))):
        for ct in range(CT):
            mm = Q.put("pe", lambda e, ct=ct, n=n, src=src: e.matmul(
                misc[n][:, 0:NX], sg[:, 0:P], src[:, ct, 0:NX], start=ct == 0, stop=ct == CT - 1),
                [tok, misc_free[n], ones_tok], "setb_pe" if ct == CT - 1 else None)
        misc_free[n] = Q.put("act", lambda e, n=n, dst=dst: e.activation(dst[:, :], misc[n][:, 0:NX], ACT.Copy),
                             [mm], "setb_act")
    tok = Q.put("act", lambda e: e.activation(a_neg[:, :], state_cols[:, 1:2], ACT.Tanh), [sc_tok], "setb_act")
    set_tok = Q.put("dve", lambda e: e.tensor_scalar(a_neg[:, :], a_neg[:, :], -1.0, None, ALU.mult),
                    [tok], "setb_dve")
    for e in Q.q:
        for tk in [w_in_tok, w_out_tok, wconv_tok, temb_tok, sc_tok, mask_tok, set_tok] + aff_tok + cols_tok:
            Q.wait(e, tk)
    barrier(Q, "b2")

    F = {}
    par_ready = [None, None]
    xhl_tok = {}
    cexp_free, cexp_ready = [None, None], [None, None]
    scan_free = [None, None]
    last_decay = [None]
    cd_tok = {}

    def prepare(i):
        t0, par_i = i * TOK, i % 2
        for hb in range(2):
            b0 = hb * HB
            x_tok = Q.dma(x2T[:, 0, :, :], d["x2T"][0:P, b0:b0 + HB, t0:t0 + TOK],
                          [F.get("x2T")], "ldb_x2T")
            for it in range(1, HT):
                x_tok = Q.dma(x2T[:, it, :, :], d["x2T"][it * P:(it + 1) * P, b0:b0 + HB, t0:t0 + TOK],
                              (), "ldb_x2T")
            yield
            for ct in range(CT):
                k = ct % 2
                m = PREP
                for it in range(HT):
                    mm = Q.put("pe", lambda e, it=it, ct=ct, m=m: e.matmul(
                        misc[m][:, :], w_in[:, it, ct * P:(ct + 1) * P],
                        x2T[:, it, :, :].rearrange("p b q -> p (b q)"), start=it == 0, stop=it == HT - 1),
                        [x_tok, misc_free[m]], "xr_pe" if it == HT - 1 else None)
                    if it % 2:
                        yield
                if ct == CT - 1:
                    F["x2T"] = mm
                hl = Q.put("act", lambda e, ct=ct, k=k, b0=b0: e.activation(
                    xr[:, k, :, 0:TAPS - 1], halo[:, ct, b0:b0 + HB, :], ACT.Copy), [F.get(("xr", k))], "xr_act")
                for bb in range(HB):
                    ev = Q.put("act", lambda e, ct=ct, k=k, bb=bb, b0=b0, m=m: e.activation(
                        xr[:, k, bb, TAPS - 1:], misc[m][:, bb * TOK:(bb + 1) * TOK], ACT.Identity,
                        bias=temb[:, ct, b0 + bb:b0 + bb + 1]), [mm], "xr_act")
                misc_free[m] = ev
                tap = Q.put("act", lambda e, ct=ct, k=k: e.activation(
                    cv[:, k, :, :], xr[:, k, :, TAPS - 1:], ACT.Copy, scale=wconv[:, ct, TAPS - 1:TAPS]),
                    [ev, F.get(("cv", k))], "xr_act")
                Q.put("act", lambda e, ct=ct, k=k, b0=b0: e.activation(
                    halo[:, ct, b0:b0 + HB, :], xr[:, k, :, TOK:TOK + TAPS - 1], ACT.Copy), [hl], "xr_act")
                halo_tok = ("xr_act", Q.count["xr_act"])
                yield
                for j in range(TAPS - 1):
                    tap = Q.put("dve", lambda e, ct=ct, k=k, j=j: e.scalar_tensor_tensor(
                        cv[:, k, :, :], xr[:, k, :, j:j + TOK], wconv[:, ct, j:j + 1], cv[:, k, :, :],
                        ALU.mult, ALU.add), [tap], "conv_dve")
                    if j < TAPS - 2:
                        yield
                F[("xr", k)] = [tap, halo_tok]
                yield
                xc_tok = F[("cv", k)] = Q.put("act", lambda e, ct=ct, k=k: e.activation(
                    xc[:, ct, :, :], cv[:, k, :, :], ACT.Silu, bias=cols[:, 2, ct:ct + 1]),
                    [tap, F.get("xc")], "silu_act")
            yield

            def tokens_first(bb, half):
                m = PREP
                for c in range(4):
                    ct = half * 4 + c
                    tr = Q.put("pe", lambda e, c=c, ct=ct, m=m: e.transpose(
                        misc[m][:, c * P:(c + 1) * P], xc[:, ct, bb, :], ident[:, :]),
                        [xc_tok, misc_free[m]], "xc_pe" if c == 3 else None)
                return m, tr
            for bb in range(HB):
                for half in range(2):
                    m, tr = tokens_first(bb, half)
                    misc_free[m] = bn = Q.put("dve", lambda e, m=m, half=half, bb=bb: e.bn_stats(
                        st6[:, bb % 2, half, :], misc[m][:, :]), [tr], "bn_dve")
                    yield
                ag = Q.put("dve", lambda e, bb=bb: e.bn_aggr(
                    mvb[:, bb, :], st6[:, bb % 2, :, :].rearrange("p a b -> p (a b)")), [bn], "bn_dve")
            tok = Q.put("dve", lambda e: e.tensor_scalar(rs[:, :], mvb[:, :, 1], EPS_LN, None, ALU.add),
                        [ag, F.get("rs")], "bn_dve")
            tok = Q.put("act", lambda e: e.activation(rs[:, :], rs[:, :], ACT.Sqrt), [tok], "bn_act")
            yield
            tok = Q.put("dve", lambda e: e.reciprocal(rs[:, :], rs[:, :]), [tok], "bn_dve")
            nm_tok = Q.put("dve", lambda e: e.tensor_scalar(nm[:, :], mvb[:, :, 0], -1.0, None, ALU.mult),
                           (), "bn_dve")
            rs_tok = Q.put("dve", lambda e: e.tensor_tensor(nmr[:, :], nm[:, :], rs[:, :], ALU.mult),
                           [tok, nm_tok], "bn_dve")
            yield
            for bb in range(HB):
                m = PREP
                for ct in range(CT):
                    mm = Q.put("pe", lambda e, ct=ct, bb=bb, m=m: e.matmul(
                        misc[m][:, 0:NX], xc[:, ct, bb, :], wx[:, ct, :], start=ct == 0, stop=ct == CT - 1),
                        [xc_tok, misc_free[m]], "proj_pe" if ct == CT - 1 else None)
                yield
                tok = Q.put("dve", lambda e, bb=bb, m=m: e.scalar_tensor_tensor(
                    proj[:, bb, :], gw[:, :], nm[:, bb:bb + 1], misc[m][:, 0:NX], ALU.mult, ALU.add),
                    [mm, rs_tok, F.get("proj")], "proj_dve")
                misc_free[m] = tok
                pr_tok = Q.put("dve", lambda e, bb=bb: e.scalar_tensor_tensor(
                    proj[:, bb, :], proj[:, bb, :], rs[:, bb:bb + 1], bw[:, :], ALU.mult, ALU.add),
                    [tok], "proj_dve")
            for bb in range(HB):
                b, k = b0 + bb, bb % 2
                for half in range(2):
                    m, tr = tokens_first(bb, half)
                    misc_free[m] = nt = Q.put("act", lambda e, m=m, half=half, bb=bb, k=k: e.activation(
                        xn[:, k, half * BANK:(half + 1) * BANK], misc[m][:, :], ACT.Identity,
                        bias=nmr[:, bb:bb + 1], scale=rs[:, bb:bb + 1]), [tr, F.get(("xn", k))], "xn_act")
                    yield
                tok = Q.put("pool", lambda e, k=k: e.tensor_tensor(xn[:, k, :], xn[:, k, :], affine[:, 0, :],
                                                                   ALU.mult), [nt], "xn_pool")
                yield
                tok = Q.put("pool", lambda e, k=k: e.tensor_tensor(xn[:, k, :], xn[:, k, :], affine[:, 1, :],
                                                                   ALU.add), [tok], "xn_pool")
                dxt = Q.put("pool", lambda e, k=k: e.tensor_tensor(dx[:, :], xn[:, k, :], affine[:, 2, :],
                                                                   ALU.mult), [tok, F.get("dx")], "xn_pool")
                F["dx"] = Q.dma(d["dx"][b, t0:t0 + TOK, :], dx[:, :], [dxt], "st_dx")
                yield
                yield
                hi = Q.put("act", lambda e, k=k: e.activation(xhi[:, :], xn[:, k, :], ACT.Copy),
                           [tok, F.get("xhi")], "xn_act")
                sqs = Q.put("act", lambda e, k=k, bb=bb: e.activation(
                    junk[:, :], xn[:, k, :], ACT.Square, accum_out=sumsq[:, bb:bb + 1]),
                    [tok, F.get("sumsq"), F.get("junk")], "xn_act")
                F["junk"] = sqs
                yield
                lo = Q.put("pool", lambda e, k=k: e.tensor_tensor(
                    xn[:, k, :].bitcast(F32R), xn[:, k, :], xhi[:, :].bitcast(F32), ALU.subtract),
                    [hi, sqs], "xn_pool")
                hi_st = Q.dma(d["xhl"][0, b, t0:t0 + TOK, :], xhi[:, :], [hi], "st_xhi")
                lo_st = Q.dma(d["xhl"][1, b, t0:t0 + TOK, :], xn[:, k, :], [lo], f"st_xlo{k}")
                F["xhi"] = [hi_st, lo]
                F[("xn", k)] = lo_st
                xhl_tok[i] = xhl_tok.get(i, []) + [hi_st, lo_st]
                yield
            F["xc"] = [("xc_pe", Q.count["xc_pe"]), ("proj_pe", Q.count["proj_pe"])]
            tok = Q.put("dve", lambda e: e.tensor_scalar(sumsq[:, :], sumsq[:, :], 1.0, None, ALU.min),
                        [sqs], "norm2_dve")
            tok = Q.put("act", lambda e: e.activation(sumsq[:, :], sumsq[:, :], ACT.Sqrt), [tok], "bn_act")
            F["rs"] = [("xn_act", Q.count["xn_act"]), pr_tok]
            yield
            for bb in range(HB):
                bt = Q.put("dve", lambda e, bb=bb: e.tensor_scalar(
                    proj[:, bb, 0:NST], proj[:, bb, 0:NST], sumsq[:, bb:bb + 1], None, ALU.mult),
                    [tok, pr_tok], "norm2_dve")
            F["sumsq"] = bt
            yield
            m = PREP
            for bb in range(HB):
                tr = Q.put("pe", lambda e, bb=bb, m=m: e.transpose(
                    misc[m][0:NX, bb * P:(bb + 1) * P], proj[:, bb, :], ident[:, :]),
                    [bt, misc_free[m]], "proj_pe" if bb == HB - 1 else None)
            F["proj"] = tr
            misc_free[m] = tok = Q.put("act", lambda e, m=m: e.activation(
                projT[:, :, :], misc[m][0:NX, :].rearrange("p (b q) -> p b q", b=HB), ACT.Copy),
                [tr, F.get("projT")], "proj_act")
            for bb in range(HB):
                for k in range(3):
                    r = (b0 + bb) * NST
                    par_tok = Q.dma(par[r:r + NST, k, :], projT[k * NST:(k + 1) * NST, bb, :],
                                    [tok, F.get("par")], "mv_par")
            F["projT"] = par_tok
            yield
        th = Q.put("act", lambda e: e.activation(par[:, 2, :], par[:, 2, :], ACT.Tanh, bias=state_cols[:, 0:1]),
                   [par_tok], "par_act")
        yield
        tok = Q.put("dve", lambda e: e.tensor_scalar(par[:, 2, :], par[:, 2, :], 0.01, a_neg[:, 0:1],
                                                     ALU.mult, ALU.mult), [th], "par_dve")
        tok = Q.put("dve", lambda e: e.tensor_scalar(par[:, 2, :], par[:, 2, :], 1.0, None, ALU.add),
                    [tok], "par_dve")
        init = 1.0 if i == 0 else decay[:, 1 - par_i, TOK - 1:TOK]
        dec = Q.put("dve", lambda e: e.tensor_tensor_scan(
            decay[:, par_i, :], par[:, 2, :], zeros[:, :], init, ALU.mult, ALU.add), [tok, last_decay[0]], "par_dve")
        last_decay[0] = dec
        yield
        tok = Q.put("dve", lambda e: e.reciprocal(inv[:, :], decay[:, par_i, :]), [dec], "par_dve")
        Q.put("dve", lambda e: e.tensor_tensor(bd[:, par_i, :], par[:, 0, :], inv[:, :], ALU.mult),
              [tok, scan_free[par_i]], "par_dve")
        Q.put("dve", lambda e: e.tensor_scalar(lim[:, par_i, 0, :], inv[:, :], 10.0, None, ALU.mult), (), "par_dve")
        par_ready[par_i] = Q.put("dve", lambda e: e.tensor_scalar(
            lim[:, par_i, 1, :], inv[:, :], -10.0, None, ALU.mult), (), "par_dve")
        cd_tok[i] = F["par"] = Q.put("dve", lambda e: e.tensor_tensor(
            cd[:, par_i, :], par[:, 1, :], decay[:, par_i, :], ALU.mult), [dec], "par_dve")
        yield
        for _ in expand(i, 0):
            yield

    junk = sb("junk", [P, DIN], mybir.dt.bfloat16)

    def expand(i, h):
        A = HC // 8
        src = cd[:, i % 2, h * HC:(h + 1) * HC].rearrange("p (a j) -> p a j", j=8)
        for a in range(A):
            cexp_ready[h] = Q.put("pool", lambda e, a=a: e.tensor_tensor(
                cexp[:, h, a * 8:(a + 1) * 8, :], src[:, a, :].unsqueeze(2).broadcast_to([P, 8, 32]),
                mask[:, :, :], ALU.mult), [cd_tok[i], cexp_free[h]], "cexp_pool")
            yield

    sx_free, sx_tok = [None] * 3, {}
    xps_free, xps_ready = [None, None], {}
    yps_free, ysb_free = [None, None], [None, None]
    g_tok, g_free = {-1: None}, [None] * 4
    y_st = {}

    def load_unit(n):
        s, ts = n % 3, n * UNIT
        toks = xhl_tok[ts // TOK]
        for j in range(4):
            w = UNIT // 4
            sx_tok[n] = Q.dma(sx[32 * j:32 * j + 2 * B, s, :, :],
                              d["xhl"][:, :, ts + j * w:ts + (j + 1) * w, :].rearrange("h b t c -> (h b) t c"),
                              [toks, sx_free[s]], f"ld_sx{s}")

    def spread_x(tm):
        n, r = divmod(tm, UNIT)
        j, w = divmod(r, UNIT // 4)
        m = tm % 2
        for half in range(2):
            xps_ready[tm] = Q.put("pe", lambda e, half=half: e.matmul(
                xps[m][:, half * BANK:(half + 1) * BANK], spread[32 * j:32 * j + 2 * B, :],
                sx[32 * j:32 * j + 2 * B, n % 3, w, half * BANK:(half + 1) * BANK], start=True, stop=True),
                [sx_tok[n], xps_free[m]], "xps_pe" if half else None)
        if r == UNIT - 1:
            sx_free[n % 3] = xps_ready[tm]

    def step(tm):
        i, tl = divmod(tm, TOK)
        pi, s = i % 2, tm % 4
        q = Q.put("dve", lambda e: e.scalar_tensor_tensor(
            g[:, s, :], xps[tm % 2][:, :], bd[:, pi, tl:tl + 1], g[:, (tm - 1) % 4, :], ALU.mult, ALU.add),
            [xps_ready[tm], g_tok[tm - 1], par_ready[pi], g_free[s]], "scan_dve")
        xps_free[tm % 2] = q
        return q

    def clip(tm, q):
        i, tl = divmod(tm, TOK)
        pi, s = i % 2, tm % 4
        g_tok[tm] = Q.put("dve", lambda e: e.tensor_scalar(
            g[:, s, :], g[:, s, :], lim[:, pi, 0, tl:tl + 1], lim[:, pi, 1, tl:tl + 1], ALU.min, ALU.max),
            [q], "scan_dve")
        if tl == TOK - 1:
            scan_free[pi] = g_tok[tm]

    def outputs(tm):
        n, slot = tm // UNIT, tm % UNIT // 2
        m = n % 2
        for tp in range(2):
            h, tc = divmod((tm + tp) % TOK, HC)
            for half in range(2):
                j = 2 * tp + half
                tok = Q.put("pe", lambda e, tp=tp, half=half, j=j, h=h, tc=tc: e.matmul(
                    yps[m][32 * j:32 * (j + 1), :], cexp[:, h, tc, :],
                    g[:, (tm + tp) % 4, half * BANK:(half + 1) * BANK], start=slot == 0, stop=slot == 3),
                    [g_tok[tm + tp], cexp_ready[h], yps_free[m]], "y_pe" if j == 3 else None)
        g_free[tm % 4] = g_free[(tm + 1) % 4] = tok
        cexp_free[h] = tok
        if slot == 3:
            yps_free[m] = ev = Q.put("act", lambda e: e.activation(ysb[:, m, :], yps[m][:, :], ACT.Copy),
                                     [tok, ysb_free[m]], "y_act")
            ysb_free[m] = Q.dma(d["y"][n], ysb[:, m, :], [ev], f"st_y{m}")
            y_st[n // (TOK // UNIT)] = [("st_y0", Q.count["st_y0"]), ("st_y1", Q.count.get("st_y1", 0))]

    def finish(i):
        t0 = i * TOK
        n0 = i * (TOK // UNIT)
        for b in range(B):
            gx_tok = Q.dma(x2T_t[:, :, :], d["x2T"][:, b, t0:t0 + TOK].rearrange("(t p) q -> p t q", p=P),
                           [F.get("x2T_t")], "ldf_x2T")
            dx_tok = Q.dma(dx_t[:, :], d["dx"][b, t0:t0 + TOK, :],
                           [("st_dx", dx_count[i]), F.get("dx_t")], "ldf_dx")
            x2_tok = Q.dma(x2_t[:, :], d["x2"][b, t0:t0 + TOK, :], [F.get("x2_t")], "ldf_x2")
            yv = d["y"][n0:n0 + TOK // UNIT].rearrange("k (u h s b) c -> h k s u b c", u=2, h=2, b=B)
            for half in range(2):
                for kk in range(TOK // UNIT):
                    y_tok = Q.dma(y_t[kk * UNIT:(kk + 1) * UNIT, half * BANK:(half + 1) * BANK],
                                  yv[half, kk, :, :, b, :], [y_st[i], F.get("y_t")], "ldf_y")
            yield
            for half in range(2):
                m = FIN
                for it in range(HT):
                    mm = Q.put("pe", lambda e, it=it, half=half, m=m: e.matmul(
                        misc[m][:, :], x2T_t[:, it, :], w_in[:, it, DIN + half * BANK:DIN + (half + 1) * BANK],
                        start=it == 0, stop=it == HT - 1), [gx_tok, misc_free[m]],
                        "gate_pe" if it == HT - 1 else None)
                    if it % 2:
                        yield
                misc_free[m] = sgt = Q.put("act", lambda e, half=half, m=m: e.activation(
                    sg[:, half * BANK:(half + 1) * BANK], misc[m][:, :], ACT.Silu), [mm, F.get("sg")], "gate_act")
            F["x2T_t"] = mm
            tok = Q.put("pool", lambda e: e.tensor_tensor(y_t[:, :], y_t[:, :], dx_t[:, :], ALU.add),
                        [y_tok, dx_tok], "yg_pool")
            F["dx_t"] = tok
            yield
            tok = Q.put("pool", lambda e: e.tensor_tensor(y_t[:, :], y_t[:, :], sg[:, :], ALU.mult),
                        [tok, sgt], "yg_pool")
            F["sg"] = tok
            yield
            yield
            for half in range(2):
                m = FIN
                for c in range(4):
                    ct = half * 4 + c
                    tr = Q.put("pe", lambda e, c=c, ct=ct, m=m: e.transpose(
                        misc[m][:, c * P:(c + 1) * P], y_t[:, ct * P:(ct + 1) * P], ident[:, :]),
                        [tok, misc_free[m]], "yg_pe" if c == 3 else None)
                misc_free[m] = cp = Q.put("act", lambda e, half=half, m=m: e.activation(
                    ygT[:, half * 4:(half + 1) * 4, :], misc[m][:, :].rearrange("p (t q) -> p t q", t=4),
                    ACT.Copy), [tr, F.get("ygT")], "yg_act")
                yield
            F["y_t"] = tr
            m = FIN
            for ct in range(CT):
                mm = Q.put("pe", lambda e, ct=ct, m=m: e.matmul(
                    misc[m][:, :], ygT[:, ct, :], w_out[:, ct, :], start=ct == 0, stop=ct == CT - 1),
                    [cp, misc_free[m]], "out_pe" if ct == CT - 1 else None)
                if ct % 2:
                    yield
            F["ygT"] = mm
            misc_free[m] = tok = Q.put("dve", lambda e, m=m: e.tensor_tensor(
                x2_t[:, :], misc[m][:, :], x2_t[:, :], ALU.add), [mm, x2_tok], "out_dve")
            F["x2_t"] = Q.dma(d["out"][b, t0:t0 + TOK, :], x2_t[:, :], [tok], "st_out")
            yield

    dx_count = {}
    count = {"prep": 0}
    for _ in prepare(0):
        count["prep"] += 1
    dx_count[0] = Q.count["st_dx"]
    for n in range(3):
        load_unit(n)
    fin_steps = B * 16
    TT_ALL = NCH * TOK
    spread_x(0)
    for i in range(NCH):
        prep, fin = Background(), Background()
        prep.add(expand(i, 1))
        if i + 1 < NCH:
            prep.add(prepare(i + 1))
        if i > 0:
            fin.add(finish(i - 1))
        quota = {"prep": 0.0, "fin": 0.0}
        for tl in range(TOK):
            tm = i * TOK + tl
            if tm + 1 < TT_ALL:
                spread_x(tm + 1) if (tm + 1) // UNIT in sx_tok else None
            q = step(tm)
            clip(tm, q)
            if tm % 2 == 1:
                outputs(tm - 1)
            if tl % UNIT == UNIT - 1 and (tm + 1) // UNIT + 2 < TT_ALL // UNIT:
                nu = (tm + 1) // UNIT + 2
                if nu * UNIT // TOK != i and nu * UNIT // TOK not in dx_count:
                    prep.finish()
                    dx_count[i + 1] = Q.count["st_dx"]
                load_unit(nu)
            quota["prep"] += (count["prep"] + 10) / (TOK - 3 * UNIT)
            quota["fin"] += fin_steps / (TOK - 2)
            for name, lane in (("prep", prep), ("fin", fin)):
                whole = int(quota[name])
                quota[name] -= whole
                lane.advance(whole)
        prep.finish()
        fin.finish()
    for _ in finish(NCH - 1):
        pass
    for e in Q.q:
        Q.wait(e, ("st_out", Q.count["st_out"]))
    ctx.close()


def program(nc, d, dims, only_attention=False):
    ctx = ExitStack()
    with ctx:
        Q = Queues(nc, ctx)
        sb = lambda n, s, dt=F32: ctx.enter_context(nc.sbuf_tensor(n, s, dt))
        t = {"ident": sb("ident", [P, P]), "ones32": sb("ones32", [P, 32])}
        ident, ones32 = t["ident"], t["ones32"]
        tok = Q.put("pool", lambda e: e.memset(ident[:, :], 0.0), signal="const_pool")
        Q.put("pool", lambda e: e.affine_select(out=ident[:, :], in_=ident[:, :], compare_op=ALU.not_equal, fill=1.0,
                                                base=0, pattern=[[-1, P]], channel_multiplier=1), [tok], "const_pool")
        tok = Q.put("pool", lambda e: e.memset(ones32[:, :], 1.0), signal="const_pool")
        Q.wait("pe", tok)
        attention_part(nc, Q, t, d, dims)
        if not only_attention:
            scan_part(nc, Q, t, d, dims)
        Q.emit()


_NAMES = ("x", "cond_2048", "L0_cond_q_weight", "L0_cond_k_weight", "L0_cond_v_weight", "L0_cond_w_weight",
          "L0_cond_u_weight", "L1_cond_W_in", "L1_cond_W_conv", "L1_cond_b_conv", "L1_cond_ln_g", "L1_cond_ln_b",
          "L1_cond_W_xproj", "L1_cond_W_dt", "L1_cond_b_dt", "L1_cond_A_log", "L1_cond_D", "L1_cond_W_out")


def kernel(**inputs):
    import concourse.bacc as bacc
    from concourse.bass_utils import run_bass_kernel_spmd

    nc = bacc.Bacc("TRN2", target_bir_lowering=False, num_devices=1)
    (x, cond, wq, wk, wv, ww, wu, w_in, w_conv, b_conv, ln_g, ln_b, w_x, w_dt, b_dt, a_log, dd, w_out) = (
        np.asarray(inputs[k]) for k in _NAMES)
    B, S = x.shape[:2]
    columns = lambda v: v.reshape(-1, P).T
    r, c = np.arange(P)[:, None], np.arange(P)[None, :]
    spread = ((r % 32 < 2 * B) & (r % 32 % B == c // NST)).astype(np.float32)
    j, m = np.arange(8)[None, :, None], np.arange(32)[None, None, :]
    mask = ((m // B == j // 2) & (m % B == r[:, :, None] // NST)).astype(np.float32).reshape(P, 8 * 32)
    given = {
        "x": x, "cond": cond, "condT": cond.T, "wqT": wq.T, "wkT": wk.T, "wvT": wv.T, "wwT": ww.T, "wuT": wu.T,
        "w_inT": w_in.T, "w_conv": w_conv.reshape(DIN, -1), "b_conv_cols": columns(b_conv), "ln_g": ln_g,
        "ln_b": ln_b, "ln_g_cols": columns(ln_g), "ln_b_cols": columns(ln_b), "wx": w_x, "wxT": w_x.T,
        "w_dtT": w_dt.T, "state_cols": np.stack([np.tile(b_dt, B), np.tile(a_log, B)], axis=1), "D": dd,
        "w_outT": w_out.T, "spread": spread, "mask": mask,
    }
    arrays, d = {}, {}
    for name, a in given.items():
        a = np.ascontiguousarray(a)
        arrays[f"in_{name}"] = a
        d[name] = nc.dram_tensor(f"in_{name}", a.shape, mybir.dt.from_np(a.dtype), kind="ExternalInput").ap()
    for name, shape, dt in (("rows", (B, 3, HID), F32), ("x2", (B, S, HID), F32), ("x2T", (HID, B, S), F32),
                            ("dx", (B, S, DIN), F32), ("xhl", (2, B, S, DIN), F32R),
                            ("y", (S // 8, P, BANK), F32)):
        d[name] = nc.dram_tensor(f"scratch_{name}", shape, dt, kind="Internal").ap()
    d["out"] = nc.dram_tensor("out", (B, S, HID), F32, kind="ExternalOutput").ap()
    program(nc, d, {"B": B, "S": S})
    return run_bass_kernel_spmd(nc, [arrays], core_ids=[0]).results[0]["out"]
```

```python
from contextlib import ExitStack

import numpy as np

import concourse.bass as bass
from concourse import mybir

F32 = mybir.dt.float32
F32R = mybir.dt.float32r
ACT = mybir.ActivationFunctionType
ALU = mybir.AluOpType
AX = mybir.AxisListType

P = 128
HID = 512
HEADS = 16
DH = HID // HEADS
GH = P // DH
GROUPS = HEADS // GH
HT = HID // P
DIN = 1024
CT = DIN // P
NST = 16
EPS_LN = 1e-5
EPS_DEMOD = 1e-8
BANK = 512
MATMUL = 0.86


class Queues:

    def __init__(self, nc, ctx):
        self.nc, self.ctx = nc, ctx
        self.q = {e: [] for e in ("pe", "act", "dve", "pool", "sp")}
        self.sems, self.count = {}, {}
        self.waited = {e: {} for e in self.q}

    def put(self, engine, make, after=(), signal=None, dma=False):
        for token in after:
            for tk in token if isinstance(token, list) else [token]:
                self.wait(engine, tk)
        if signal is None:
            self.q[engine].append(make)
            return None
        if signal not in self.sems:
            self.sems[signal] = self.ctx.enter_context(self.nc.semaphore(signal))
            self.count[signal] = 0
        sem, by = self.sems[signal], 16 if dma else 1
        self.count[signal] += by
        self.q[engine].append(lambda e: make(e).then_inc(sem, by))
        return signal, self.count[signal]

    def wait(self, engine, token):
        if token is None:
            return
        name, value = token
        if self.waited[engine].get(name, 0) >= value:
            return
        self.waited[engine][name] = value
        sem = self.sems[name]
        self.q[engine].append(lambda e: e.wait_ge(sem, value))

    def dma(self, out, in_, after=(), signal=None, engine="sp"):
        out, in_ = (a.bitcast(F32) if a.dtype == F32R else a for a in (out, in_))
        return self.put(engine, lambda e: e.dma_start(out, in_), after, signal, dma=True)

    def emit(self):
        with self.nc.Block() as block:
            for name, reg in (("pe", block.tensor), ("act", block.scalar), ("dve", block.vector),
                              ("pool", block.gpsimd), ("sp", block.sync)):
                def body(e, name=name):
                    for f in self.q[name]:
                        f(e)
                reg(body)


class Lanes:

    def __init__(self):
        self.lanes, self.now, self.work, self.pool = [], 0.0, 0.0, 0.0

    def add(self, gen, after=None):
        lane = {"gen": gen, "clock": self.now, "after": after, "left": True, "reply": None}
        self.lanes.append(lane)
        return lane

    def piece(self, lane):
        try:
            work, pause, pool, moment = (lane["gen"].send(lane["reply"]) + (0.0, None))[:4]
        except StopIteration:
            lane["left"] = False
            return
        self.work -= work
        if pool:
            self.pool = max(self.pool, self.now) + pool
        lane["reply"] = self.pool
        lane["clock"] = max(lane["clock"], self.now - 2.3, (moment or 0.0) + 0.5) + pause

    def advance(self, time, work):
        self.now += time
        self.work = min(self.work + work, 1.2)
        for lane in self.lanes:
            while (lane["left"] and lane["clock"] <= self.now and self.work > 0
                   and not (lane["after"] and lane["after"]["left"])):
                self.piece(lane)

    def finish(self, which, enough=lambda: False):
        for lane in which:
            while lane["left"] and not enough():
                self.piece(lane)


def barrier(Q, name):
    tokens = []
    for e in ("pe", "act", "dve", "pool", "sp"):
        tokens.append(Q.put(e, lambda en: en.nop(), signal=f"{name}_{e}"))
    for e in Q.q:
        for t in tokens:
            Q.wait(e, t)


def attention_part(nc, Q, t, d, dims):
    B, S = dims["B"], dims["S"]
    TT = S // P
    QC = min(BANK, S)
    NQ = S // QC
    SCALE = float(DH) ** -0.5
    stack = ExitStack()
    sb = lambda n, s, dt=F32: stack.enter_context(nc.sbuf_tensor(n, s, dt))
    pb = lambda n, s, dt=F32: stack.enter_context(nc.psum_tensor(n, s, dt))

    ident, ones32 = t["ident"], t["ones32"]
    wv = sb("wv", [P, HT, HID])
    qk_dc = sb("qk_dc", [P, 2, HT, B])
    rstd = sb("rstd", [P, B * TT])
    nmr = sb("nmr", [P, B * TT])
    misc = [pb(f"misc{i}", [P, BANK]) for i in range(2)]
    misc_free = [None, None]
    GROUP, BATCH = 0, 1

    setup = ExitStack()
    sbs = lambda n, s, dt=F32: setup.enter_context(nc.sbuf_tensor(n, s, dt))
    wsq = sbs("wsq", [P, 5, HT, HID])
    condT = sbs("condT_sb", [P, 2 * HT, B])
    s2row = sbs("s2row", [B, HID])
    rows = sbs("rows", [B, 3, HID])
    s1b = sbs("s1b", [P, 2, HID])
    xin = sbs("xin_s", [P, 4, HID])
    xms = sbs("xm_s", [P, 2, HID])
    bst = sbs("bst", [P, 2, 6])
    mv = sbs("mv", [P, B * TT, 2])

    cond_in = Q.dma(condT[:, :, :], d["condT"].rearrange("(t p) b -> p t b", p=P), signal="ld_cond")
    s2_in = Q.dma(s2row[:, :], d["cond"][:, HID:2 * HID], signal="ld_s2")
    w_in = [Q.dma(wsq[:, n, :, :], d[w].rearrange("(t p) o -> p t o", p=P), signal=f"ld_w{n}")
            for n, w in enumerate(("wqT", "wkT", "wvT", "wwT", "wuT"))]
    wv_in = Q.dma(wv[:, :, :], d["wvT"].rearrange("(t p) o -> p t o", p=P), signal="ld_wv")
    cond_sq = Q.put("act", lambda e: e.activation(condT[:, :, :], condT[:, :, :], ACT.Square),
                    [cond_in], "setup_act")
    sq = [Q.put("act", lambda e, n=n: e.activation(wsq[:, n, :, :], wsq[:, n, :, :], ACT.Square),
                [w_in[n]], "setup_act") for n in range(5)]
    for n in range(2):
        for ot in range(HT):
            for it in range(HT):
                last = (n == 1 and ot == HT - 1 and it == HT - 1)
                c = (n * HT + ot) * B
                tok = Q.put("pe", lambda e, n=n, ot=ot, it=it, c=c: e.matmul(
                    misc[0][:, c:c + B], wsq[:, n, it, ot * P:(ot + 1) * P], condT[:, it, :],
                    start=it == 0, stop=it == HT - 1), [cond_sq, sq[n]], "setup_pe" if last else None)
    flat = qk_dc[:, :, :, :].rearrange("p n o b -> p (n o b)")
    tok = Q.put("dve", lambda e: e.tensor_scalar(flat, misc[0][:, 0:2 * HT * B], EPS_DEMOD, None, ALU.add),
                [tok], "setup_dve")
    qk_free = tok
    tok = Q.put("act", lambda e: e.activation(flat, flat, ACT.Sqrt), [tok], "setup_act")
    qk_ready = Q.put("dve", lambda e: e.reciprocal(flat, flat), [tok], "setup_dve")
    bank_free = [qk_free, None]
    row_tok = None
    for j, n in enumerate((2, 3, 4)):
        m = (j + 1) % 2
        h0 = 0 if n == 2 else HT
        for it in range(HT):
            tok = Q.put("pe", lambda e, n=n, it=it, m=m, h0=h0: e.matmul(
                misc[m][0:B, :], condT[:, h0 + it, :], wsq[:, n, it, :], start=it == 0, stop=it == HT - 1),
                [sq[n], bank_free[m]], "setup_pe" if it == HT - 1 else None)
        tok = Q.put("dve", lambda e, j=j, m=m: e.tensor_scalar(rows[:, j, :], misc[m][0:B, :], EPS_DEMOD, None,
                                                               ALU.add), [tok], "setup_dve")
        bank_free[m] = tok
        row_tok = Q.put("act", lambda e, j=j: e.activation(rows[:, j, :], rows[:, j, :], ACT.Sqrt),
                        [tok], "setup_act")
    tok = Q.put("dve", lambda e: e.reciprocal(rows[:, :, :], rows[:, :, :]), [row_tok], "setup_dve")
    tok = Q.put("dve", lambda e: e.tensor_tensor(rows[:, 0, :], rows[:, 0, :], s2row[:, :], ALU.mult),
                [tok, s2_in], "setup_dve")
    rows_out = Q.dma(d["rows"], rows[:, :, :], [tok], "st_rows")
    s1_free, x_free, xm_free = [None] * 2, [None] * 4, [None] * 2
    st_tok = None
    for b in range(B):
        s1_in = Q.dma(s1b[:, b % 2, :], d["cond"][b, 0:HID].partition_broadcast(P), [s1_free[b % 2]],
                      f"ld_s1_{b % 2}")
        for tt in range(TT):
            i = b * TT + tt
            x_in = Q.dma(xin[:, i % 4, :], d["x"][b, tt * P:(tt + 1) * P, :], [x_free[i % 4]], f"ld_xs{i % 4}")
            mul = Q.put("pool", lambda e, i=i, b=b: e.tensor_tensor(
                xms[:, i % 2, :], xin[:, i % 4, :], s1b[:, b % 2, :], ALU.mult),
                [x_in, s1_in, xm_free[i % 2]], "stat_pool")
            x_free[i % 4] = s1_free[b % 2] = mul
            tok = Q.put("dve", lambda e, i=i: e.bn_stats(bst[:, i % 2, :], xms[:, i % 2, :]), [mul], "stat_dve")
            xm_free[i % 2] = tok
            st_tok = Q.put("dve", lambda e, i=i: e.bn_aggr(mv[:, i, :], bst[:, i % 2, :]), [tok], "stat_dve")
    tok = Q.put("dve", lambda e: e.tensor_scalar(rstd[:, :], mv[:, :, 1], EPS_LN, None, ALU.add),
                [st_tok], "stat_dve")
    tok = Q.put("act", lambda e: e.activation(rstd[:, :], rstd[:, :], ACT.Sqrt), [tok], "stat_act")
    tok = Q.put("dve", lambda e: e.reciprocal(rstd[:, :], rstd[:, :]), [tok], "stat_dve")
    stats_ready = Q.put("dve", lambda e: e.scalar_tensor_tensor(
        nmr[:, :], mv[:, :, 0], -1.0, rstd[:, :], ALU.mult, ALU.mult), [tok], "stat_dve")
    for e in ("pe", "act", "dve", "pool", "sp"):
        for tk in (stats_ready, qk_ready, rows_out, wv_in):
            Q.wait(e, tk)
    barrier(Q, "b0")
    setup.close()

    GROUP_STEP = (6.6, 5.6, 5.6, 6.6)
    wqk = sb("wqk", [P, 2, HT, P])
    wwu = sb("wwu", [P, 2, HT, HID])
    xhT = sb("xhT", [P, HT, S])
    V012 = sb("V012", [P, TT, 3 * P])
    V3 = sb("V3", [P, 2, TT, P])
    acc = sb("acc", [P, 2, GH, QC])
    qhat = sb("qhat", [P, 2, GH, S], F32R)
    khat = sb("khat", [P, 2, GH, S], F32R)
    halves = sb("halves", [P, 2, 2, QC], F32R)
    ORDER = (1, 1, 0, 0, 1, 0, 1)
    PICK = ((4, 3), (0, 2))
    pick = sb("pick", [P, GH, len(ORDER), DH], F32R)
    prob = sb("prob", [P, 2 * GH, QC])
    aoT = sb("aoT", [P, GROUPS, S])
    xt = sb("xt", [P, 2, HID])
    xh = sb("xh", [P, HID])
    brow = sb("brow", [P, 4, HID])
    mx2 = sb("mx2", [P, GH * TT, NQ])
    mx = sb("mx", [P, GH * TT])
    mrow = sb("mrow", [GH * TT, 2, P], F32R)
    rsum = sb("rsum", [P, QC])
    smax = [pb(f"smax{i}", [P, BANK]) for i in range(2)]
    sexp = [pb(f"sexp{i}", [P, BANK]) for i in range(2)]
    av = [pb(f"av{i}", [P, BANK]) for i in range(2)]

    for k, one in enumerate(ORDER):
        pick_tok = Q.put("dve", lambda e, k=k, one=one: e.tensor_scalar(
            pick[:, :, k, :], ident[:, :].rearrange("p (h d) -> p h d", h=GH), float(one), None, ALU.mult), signal="kones")
    ones_tok = None
    for i in range(2):
        ones_tok = Q.put("dve", lambda e, i=i: e.memset(khat[96:98, i, :, :].bitcast(F32), 1.0), signal="kones")

    smax_free, sexp_free = [None] * 2, [None] * 2
    prob_free = [None] * (2 * GH)
    prob_done = [None] * (2 * GH)
    hat_free = [None, None]
    hat_tok = [None, None]
    mrow_tok = [None, None]
    halves_free = [None] * 2
    rsum_free = [None]
    xhT_free, xhT_ready = [None], [None]
    V_ready = [None, None]
    V_free = {}
    acc_free, acc_tok = [None, None], [[None] * GH for _ in range(2)]
    av_free = [None, None]
    brow_tok, brow_free = [None], [None]
    wwu_ready, wwu_free = [None, None], [None, None]
    aoT_free = [None] * 1
    aoT_ready = {}
    xt_free = [None, None]
    xh_free = [None]
    wqk_ready, wqk_free = {}, [None]
    xt_turn = [0]

    def load_group_weights(u):
        g = u % GROUPS
        wqk_tok = [Q.dma(wqk[:, n, :, :], d[w][:, g * P:(g + 1) * P].rearrange("(t p) o -> p t o", p=P),
                      [wqk_free[0]], f"ld_wqk{n}") for n, w in enumerate(("wqT", "wkT"))]
        wqk_ready.update(enumerate(wqk_tok))

    def value(b, tt, g):
        return V3[:, b % 2, tt, :] if g == GROUPS - 1 else V012[:, tt, g * P:(g + 1) * P]

    def load_rows(tt, b, name):
        s = xt_turn[0] % 2
        xt_turn[0] += 1
        return s, Q.dma(xt[:, s, :], d[name][b, tt * P:(tt + 1) * P, :],
                        [xt_free[s]] + (xs_all[b] if name == "xs" else []), f"ld_xt{s}")

    def normalise_batch(b):
        m = BATCH
        brow_tok[0] = Q.dma(brow[:, 0, :], d["cond"][b, 0:HID].partition_broadcast(P), [brow_free[0]], "ld_brow")
        s, x_in = load_rows(0, b, "x")
        yield 0.0, 2.5
        for tt in range(TT):
            i = b * TT + tt
            mod = brow_free[0] = Q.put("pool", lambda e, s=s: e.tensor_tensor(
                xt[:, s, :], xt[:, s, :], brow[:, 0, :], ALU.mult), [x_in, brow_tok[0]], "ln_pool")
            if tt + 1 < TT:
                following = load_rows(tt + 1, b, "x")
            yield 0.0, 3.0
            nrm = xt_free[s] = Q.put("act", lambda e, i=i, s=s: e.activation(
                xh[:, :], xt[:, s, :], ACT.Identity, bias=nmr[:, i:i + 1], scale=rstd[:, i:i + 1]),
                [mod, xh_free[0]], "ln_act")
            yield 0.0, 1.2
            for it in range(HT):
                tr = Q.put("pe", lambda e, it=it: e.transpose(
                    misc[m][:, it * P:(it + 1) * P], xh[:, it * P:(it + 1) * P], ident[:, :]),
                    [nrm, misc_free[m]], "ln_pe" if it == HT - 1 else None)
            xh_free[0] = tr
            misc_free[m] = xhT_ready[0] = Q.put("act", lambda e, tt=tt: e.activation(
                xhT[:, :, tt * P:(tt + 1) * P], misc[m][:, :].rearrange("p (t q) -> p t q", t=HT), ACT.Copy),
                [tr, xhT_free[0]], "ln_act")
            s, x_in = following
            yield 0.5, 0.8

    def make_values(b):
        m = BATCH
        row_tok = Q.dma(brow[:, 1, :], d["rows"][b, 0].partition_broadcast(P), [vrow_free[0]], "ld_vrow")
        for tt in range(TT):
            for it in range(HT):
                mm = Q.put("pe", lambda e, it=it, tt=tt: e.matmul(
                    misc[m][:, :], xhT[:, it, tt * P:(tt + 1) * P], wv[:, it, :], start=it == 0, stop=it == HT - 1),
                    [xhT_ready[0], misc_free[m]], "v_pe" if it == HT - 1 else None)
                yield MATMUL, MATMUL
            yield 0.0, 1.2
            Q.put("dve", lambda e, tt=tt: e.tensor_tensor(
                V012[:, tt, :], misc[m][:, 0:3 * P], brow[:, 1, 0:3 * P], ALU.mult),
                [mm, row_tok, V_free.get((b - 1, 0)), V_free.get((b - 1, 1)), V_free.get((b - 1, 2))], "v_dve")
            misc_free[m] = V_ready[b % 2] = vrow_free[0] = Q.put("dve", lambda e, tt=tt: e.tensor_tensor(
                V3[:, b % 2, tt, :], misc[m][:, 3 * P:], brow[:, 1, 3 * P:], ALU.mult),
                [V_free.get((b - 2, 3))], "v_dve")
            yield 0.0, 1.2
        xhT_read[0] = mm

    def skip_path(b):
        m = BATCH
        for tt in range(TT):
            s, x_in = load_rows(tt, b, "x")
            for ot in range(HT):
                tr = Q.put("pe", lambda e, ot=ot, tt=tt: e.transpose(
                    misc[m][:, ot * P:(ot + 1) * P], value(b, tt, ot), ident[:, :]),
                    [V_ready[b % 2], misc_free[m]], "v_pe" if ot == HT - 1 else None)
            cp = misc_free[m] = Q.put("act", lambda e: e.activation(
                xh[:, :], misc[m][:, :], ACT.Copy), [tr, xh_free[0]], "v_act")
            yield 0.5, 1.6
            for ot in range(HT):
                mm = Q.put("pe", lambda e, ot=ot: e.matmul(
                    misc[m][:, :], xh[:, ot * P:(ot + 1) * P], wwu[:, 1, ot, :], start=ot == 0, stop=ot == HT - 1),
                    [cp, wwu_ready[1], misc_free[m]], "v_pe" if ot == HT - 1 else None)
                yield MATMUL, MATMUL
            xh_free[0] = mm
            yield 0.0, 1.2
            misc_free[m] = tok = Q.put("dve", lambda e, s=s: e.tensor_tensor(
                xt[:, s, :], misc[m][:, :], xt[:, s, :], ALU.add), [mm, x_in], "v_dve")
            yield 0.0, 1.2
            xt_free[s] = Q.dma(d["xs"][b, tt * P:(tt + 1) * P, :], xt[:, s, :], [tok], f"st_xs{s}")
            xs_all[b] = [(n, Q.count[n]) for n in ("st_xs0", "st_xs1") if n in Q.count]
        wwu_free[1] = mm
    xs_all, vrow_free, xhT_read = {}, [None], [None]

    def scale_weights(b, n):
        r_tok = Q.dma(brow[:, 2 + n, :], d["rows"][b, 1 + n].partition_broadcast(P), [wwu_ready[n]], f"ld_row{n}")
        w_tok = Q.dma(wwu[:, n, :, :], d[("wwT", "wuT")[n]].rearrange("(t p) o -> p t o", p=P), [wwu_free[n]],
                      f"ld_wwu{n}")
        yield 0.0, 4.0
        for ot in range(HT):
            wwu_ready[n] = Q.put("pool", lambda e, ot=ot: e.tensor_tensor(
                wwu[:, n, ot, :], wwu[:, n, ot, :], brow[:, 2 + n, :], ALU.mult), [w_tok, r_tok], "wu_pool")
            yield 0.0, 4.0

    def project(u):
        b, g, s = u // GROUPS, u % GROUPS, u % 2

        def lay_out(h, n, c, made):
            m = h % 2
            for half in range(2):
                at = PICK[n][half]
                tr = Q.put("pe", lambda e, half=half, at=at: e.matmul(
                    smax[m][0:96, 0:QC], pick[:, h, at:at + 3, :].rearrange("p k d -> p (k d)"), halves[:, n, half, :],
                    start=half == 0, stop=half == 1), [made, pick_tok, smax_free[m]], "pick_pe" if half else None)
            hat = (qhat, khat)[n]
            smax_free[m] = hat_tok[s] = Q.put("act", lambda e: e.activation(
                hat[0:96, s, h, c * QC:(c + 1) * QC], smax[m][0:96, 0:QC], ACT.Copy),
                [tr, hat_free[s]], "pick_act")
            halves_free[n] = tr
        before = None
        parts = [(c, n) for c in range(NQ) for n in range(2)]
        for part in parts + [None]:
            for it in range(HT):
                if part:
                    c, n = part
                    mm = Q.put("pe", lambda e, it=it, n=n, c=c: e.matmul(
                        misc[GROUP][:, 0:QC], wqk[:, n, it, :], xhT[:, it, c * QC:(c + 1) * QC],
                        start=it == 0, stop=it == HT - 1),
                        [xhT_ready[0], wqk_ready[n], misc_free[GROUP]], "qk_pe" if it == HT - 1 else None)
                    yield MATMUL, MATMUL
                if before:
                    lay_out(it, *before)
                    yield 0.3, 0.4 if part else 1.3
            if part:
                yield 0.0, 0.7
                dc = qk_dc[:, n, g, b:b + 1]
                hi = Q.put("act", lambda e, n=n, dc=dc: e.activation(
                    halves[:, n, 0, :], misc[GROUP][:, 0:QC], ACT.Copy, scale=dc), [mm, halves_free[n]], "qk_act")
                yield 0.0, 0.7
                lo = Q.put("dve", lambda e, n=n, dc=dc: e.scalar_tensor_tensor(
                    halves[:, n, 1, :], misc[GROUP][:, 0:QC], dc, halves[:, n, 0, :].bitcast(F32), ALU.mult,
                    ALU.subtract), [hi], "qk_dve")
                misc_free[GROUP] = lo
                before = (n, c, lo)
                yield 0.0, 1.0
        xhT_free[0] = [mm, xhT_read[0]]
        wqk_free[0] = mm
        if u + 1 < B * GROUPS:
            load_group_weights(u + 1)

    def maxima(u):
        s = u % 2
        banks = [(smax[0], smax_free, 0), (smax[1], smax_free, 1), (misc[GROUP], misc_free, GROUP)]
        for h in range(GH):
            for qt in range(TT):
                for c in range(NQ):
                    bank, free, k = banks[((h * TT + qt) * NQ + c) % 3]
                    mm = Q.put("pe", lambda e, h=h, qt=qt, c=c, bank=bank: e.matmul(
                        bank[:, 0:QC], qhat[0:96, s, h, qt * P:(qt + 1) * P],
                        khat[0:96, s, h, c * QC:(c + 1) * QC], start=True, stop=True),
                        [hat_tok[s], free[k]], "smax_pe")
                    free[k] = rd = Q.put("dve", lambda e, h=h, qt=qt, c=c, bank=bank: e.tensor_reduce(
                        mx2[:, h * TT + qt, c:c + 1], bank[:, 0:QC], AX.X, ALU.max), [mm], "smax_dve")
                    yield 0.25, 0.62
        rd = Q.put("dve", lambda e: e.tensor_reduce(mx[:, :], mx2[:, :, :], AX.X, ALU.max), [rd], "smax_dve")
        yield 0.0, 1.5
        m = GROUP
        n_rows = GH * TT
        tr = Q.put("pe", lambda e, m=m: e.transpose(misc[m][0:n_rows, 0:P], mx[:, :], ident[:, :]),
                   [rd, misc_free[m]], "mrow_pe")
        hi = Q.put("act", lambda e, m=m: e.activation(mrow[:, 0, :], misc[m][0:n_rows, 0:P], ACT.Copy, scale=-1.0),
                   [tr, mrow_tok[1 - s], mrow_tok[s]], "mrow_act")
        lo = Q.put("dve", lambda e, m=m: e.scalar_tensor_tensor(
            mrow[:, 1, :], misc[m][0:n_rows, 0:P], -1.0, mrow[:, 0, :].bitcast(F32), ALU.mult, ALU.subtract),
            [hi], "mrow_dve")
        misc_free[m] = lo
        for r in range(2):
            mrow_tok[s] = Q.dma(qhat[96 + r:97 + r, s, :, :].rearrange("p h (t q) -> p (h t) q", q=P),
                                mrow[:, r, :], [(hi, lo)[r], hat_free[s]], f"mrow{s}")
        yield 0.0, 2.0

    def finish_batch(b):
        m = BATCH
        for tt in range(TT):
            s, x_in = load_rows(tt, b, "xs")
            for ot in range(HT):
                mm = Q.put("pe", lambda e, ot=ot, tt=tt: e.matmul(
                    misc[m][:, :], aoT[:, ot, tt * P:(tt + 1) * P], wwu[:, 0, ot, :], start=ot == 0,
                    stop=ot == HT - 1), [aoT_ready[b], wwu_ready[0], misc_free[m]], "fin_pe" if ot == HT - 1 else None)
                yield MATMUL, MATMUL
            yield 0.0, 0.8
            add = misc_free[m] = Q.put("dve", lambda e, s=s: e.tensor_tensor(
                xt[:, s, :], misc[m][:, :], xt[:, s, :], ALU.add), [mm, x_in], "fin_dve")
            yield 0.0, 0.8
            for it in range(HT):
                tr = Q.put("pe", lambda e, it=it, s=s: e.transpose(
                    misc[m][:, it * P:(it + 1) * P], xt[:, s, it * P:(it + 1) * P], ident[:, :]),
                    [add, misc_free[m]], "fin_pe" if it == HT - 1 else None)
            cp = misc_free[m] = Q.put("act", lambda e: e.activation(xh[:, :], misc[m][:, :], ACT.Copy),
                                      [tr, xh_free[0]], "fin_act")
            x2_st = Q.dma(d["x2"][b, tt * P:(tt + 1) * P, :], xt[:, s, :], [add], f"st_x2_{s}")
            yield 0.5, 1.0
            st = Q.dma(d["x2T"][:, b, tt * P:(tt + 1) * P].rearrange("(t p) q -> p t q", p=P),
                       xh[:, :].rearrange("p (t q) -> p t q", t=HT), [cp], "st_x2T")
            xh_free[0] = st
            xt_free[s] = [x2_st, tr]
        wwu_free[0] = mm
        aoT_free[0] = mm

    def attend(u, lanes, step_time, first):
        b, g, s = u // GROUPS, u % GROUPS, u % 2
        need = [hat_tok[s], mrow_tok[s], ones_tok]
        steps = [(c, kt) for c in range(NQ) for kt in range(TT)]

        def score(n, h):
            c, kt = steps[n]
            bank, slot = (n * GH + h) % 2, (n % 2) * GH + h
            mm = hat_free[s] = Q.put("pe", lambda e: e.matmul(
                sexp[bank][:, 0:QC], khat[0:98, s, h, kt * P:(kt + 1) * P],
                qhat[0:98, s, h, c * QC:(c + 1) * QC], start=True, stop=True),
                need + [sexp_free[bank]], "sexp_pe")
            a = (u * NQ + c) % 2
            out, free = (acc[:, a, h, :], acc_free[a]) if kt == 0 else (prob[:, slot, :], prob_free[slot])
            prob_done[slot] = sexp_free[bank] = Q.put("act", lambda e: e.activation(
                out, sexp[bank][:, 0:QC], ACT.Exp, scale=SCALE), [mm, free], "exp_act")

        def contract(n):
            c, kt = steps[n]
            a = (u * NQ + c) % 2
            for h in range(GH):
                slot = (n % 2) * GH + h
                lhs = value(b, kt, g)[:, h * DH:(h + 1) * DH]
                rhs = acc[:, a, h, :] if kt == 0 else prob[:, slot, :]
                tok = Q.put("pe", lambda e, h=h, lhs=lhs, rhs=rhs: e.matmul(
                    av[a][h * DH:(h + 1) * DH, 0:QC], lhs, rhs, start=kt == 0, stop=kt == TT - 1),
                    [prob_done[slot], V_ready[b % 2], av_free[a]], "av_pe" if h == GH - 1 else None)
            V_free[(b, g)] = tok
            for h in range(GH):
                if kt == 0:
                    acc_tok[a][h] = tok
                else:
                    prob_free[(n % 2) * GH + h] = [tok]
            return tok

        def add_up(n):
            c, kt = steps[n]
            a = (u * NQ + c) % 2
            if kt == 0:
                return
            for h in range(GH):
                slot = (n % 2) * GH + h
                acc_tok[a][h] = Q.put("pool", lambda e, h=h, slot=slot:
                                   e.tensor_tensor(acc[:, a, h, :], acc[:, a, h, :], prob[:, slot, :], ALU.add),
                                   [prob_done[slot], acc_tok[a][h]], "acc_pool")
                prob_free[slot].append(acc_tok[a][h])

        def normalise(c, done):
            a, m = (u * NQ + c) % 2, NQ - 1
            for h in range(GH):
                sm = Q.put("pe", lambda e, h=h: e.matmul(
                    smax[m][h * DH:(h + 1) * DH, 0:QC], ones32[:, :], acc[:, a, h, :], start=True, stop=True),
                    [acc_tok[a][h], smax_free[m]], "sums_pe" if h == GH - 1 else None)
            acc_free[a] = sm
            cp = smax_free[m] = Q.put("act", lambda e: e.activation(rsum[:, :], smax[m][:, 0:QC], ACT.Copy),
                                      [sm, rsum_free[0]], "norm_act")
            rc = Q.put("dve", lambda e: e.reciprocal(rsum[:, :], rsum[:, :]), [cp], "norm_dve")
            rsum_free[0] = av_free[a] = aoT_ready[b] = Q.put("dve", lambda e: e.tensor_tensor(
                aoT[:, g, c * QC:(c + 1) * QC], av[a][:, 0:QC], rsum[:, :], ALU.mult),
                [rc, done, aoT_free[0]], "norm_dve")

        def advance():
            lanes.advance(step_time / 7, (step_time - 2 * MATMUL) / 7)
        for n in range(len(steps)):
            if n == len(steps) // 2 and first:
                lanes.finish([first])
            score(n, 0)
            advance()
            score(n, 1)
            advance()
            if n:
                done = contract(n - 1)
            advance()
            advance()
            if not n and attend.last:
                attend.last()
            score(n, 2)
            if n:
                add_up(n - 1)
                if attend.pending:
                    attend.pending()
                    attend.pending = None
                if steps[n - 1][1] == TT - 1:
                    attend.pending = lambda c=steps[n - 1][0], done=done: normalise(c, done)
            advance()
            score(n, 3)
            advance()
            advance()

        def last():
            done = contract(len(steps) - 1)
            add_up(len(steps) - 1)
            attend.pending = lambda: normalise(NQ - 1, done)
        attend.last = last
        lanes.finish(lanes.lanes)
        lanes.lanes.clear()

    def flush():
        if attend.last:
            attend.last()
        if attend.pending:
            attend.pending()
        attend.last = attend.pending = None
    attend.last = attend.pending = None

    U = B * GROUPS
    load_group_weights(0)
    for gen in (normalise_batch(0), make_values(0), project(0), maxima(0)):
        for _ in gen:
            pass
    lanes = Lanes()
    for u in range(U):
        b, g = divmod(u, GROUPS)
        first = None
        if g == 0 and b > 0:
            first = lanes.add(finish_batch(b - 1))
        if g == GROUPS - 1 and b + 1 < B:
            lanes.add(make_values(b + 1))
        if u + 1 < U:
            q = lanes.add(project(u + 1))
            lanes.add(maxima(u + 1), after=q)
        if g == 0 and b == 0:
            lanes.add(scale_weights(b, 1))
        if g == 1:
            lanes.add(skip_path(b))
        if g == GROUPS - 2:
            w = lanes.add(scale_weights(b, 0))
            if b + 1 < B:
                lanes.add(scale_weights(b + 1, 1), after=w)
                lanes.add(normalise_batch(b + 1), after=q)
        attend(u, lanes, GROUP_STEP[g], first)
    flush()
    for _ in finish_batch(B - 1):
        pass
    for name in ("st_x2_0", "st_x2_1", "st_x2T"):
        Q.wait("sp", (name, Q.count[name]))
    barrier(Q, "b1")
    stack.close()


def scan_part(nc, Q, t, d, dims):
    B, S = dims["B"], dims["S"]
    TOK = P
    NCH = S // TOK
    HB = B // 2
    UNIT = 8
    TAPS = 4
    NX = 3 * NST
    HC = TOK // 2
    ctx = ExitStack()
    sb = lambda n, s, dt=F32: ctx.enter_context(nc.sbuf_tensor(n, s, dt))
    pb = lambda n, s, dt=F32: ctx.enter_context(nc.psum_tensor(n, s, dt))
    ident = t["ident"]
    SCAN_STEP = 2.3
    STEP = 3.0

    w_in = sb("w_in", [P, HT, 2 * DIN])
    w_out = sb("w_out", [P, CT, HID])
    wx = sb("wx", [P, CT, NX])
    affine = sb("affine", [P, 3, DIN])
    gw = sb("gw", [P, NX])
    bw = sb("bw", [P, NX])
    cols = sb("cols", [P, 3, CT])
    wconv = sb("wconv", [P, CT, TAPS])
    temb = sb("temb", [P, CT, B])
    state_cols = sb("state_cols", [P, 2])
    a_neg = sb("a_neg", [P, 1])
    spread = sb("spread", [P, P], F32R)
    mask = sb("mask", [P, 8, 32])
    halo = sb("halo", [P, CT, B, TAPS - 1])
    zeros = sb("zeros", [P, TOK])
    x2T = sb("x2T_sb", [P, HT, HB, TOK])
    xr = sb("xr", [P, 2, HB, TAPS - 1 + TOK])
    cv = sb("cv", [P, 2, HB, TOK])
    xc = sb("xc", [P, CT, HB, TOK])
    st6 = sb("st6", [P, 2, 2, 6])
    mvb = sb("mvb", [P, HB, 2])
    rs = sb("rs", [P, HB])
    nm = sb("nm", [P, HB])
    nmr = sb("nmr_b", [P, HB])
    xn = sb("xn", [P, 3, DIN])
    xhi = sb("xhi", [P, 2, DIN], F32R)
    dx = sb("dx", [P, DIN])
    sumsq = sb("sumsq", [P, HB])
    proj = sb("proj", [P, 3, B, NST])
    par = sb("par", [P, 3, TOK])
    decay = sb("decay", [P, 2, TOK])
    inv = sb("inv", [P, TOK])
    bd = sb("bd", [P, 2, TOK])
    lim = sb("lim", [P, 2, 2, TOK])
    cd = sb("cd", [P, 2, TOK])
    cexp = sb("cexp", [P, 2, HC, 32])
    sx = sb("sx", [P, 2, UNIT // 4, DIN], F32R)
    g = sb("g", [P, 4, DIN])
    ysb = sb("ysb", [P, 2, BANK])
    y_t = sb("y_t", [P, DIN])
    dx_t = sb("dx_t", [P, DIN])
    sg = sb("sg", [P, DIN])
    ygT = sb("ygT", [P, CT, P])
    x2_t = sb("x2_t", [P, HID])
    x2T_t = sb("x2T_t", [P, HT, P])
    xps = [pb(f"xps{i}", [P, DIN]) for i in range(2)]
    yps = [pb(f"yps{i}", [P, BANK]) for i in range(2)]
    misc = [pb(f"miscb{i}", [P, BANK]) for i in range(2)] + yps
    misc_free = [None] * 4

    class Banks:

        def __init__(self, *banks):
            self.banks, self.n = banks, 0

        def take(self):
            self.n += 1
            return self.banks[self.n % len(self.banks)]

    ld = lambda out, in_, name: Q.dma(out, in_, (), name)
    w_in_tok = ld(w_in[:, :, :], d["w_inT"].rearrange("(t p) o -> p t o", p=P), "ldb_win")
    w_out_tok = ld(w_out[:, :, :], d["w_outT"].rearrange("(t p) o -> p t o", p=P), "ldb_wout")
    wx_tok = ld(wx[:, :, 0:2 * NST], d["wxT"].rearrange("(t p) o -> p t o", p=P)[:, :, 0:2 * NST], "ldb_wx")
    aff_tok = [ld(affine[:, n, :], d[k].partition_broadcast(P), f"ldb_a{n}") for n, k in
               enumerate(("ln_g", "ln_b", "D"))]
    cols_tok = [ld(cols[:, n, :], d[k], f"ldb_c{n}") for n, k in
                enumerate(("ln_g_cols", "ln_b_cols", "b_conv_cols"))]
    wconv_tok = ld(wconv[:, :, :], d["w_conv"].rearrange("(t p) k -> p t k", p=P), "ldb_wc")
    temb_tok = ld(temb[:, :, :], d["condT"].rearrange("(t p) b -> p t b", p=P), "ldb_te")
    sc_tok = ld(state_cols[:, :], d["state_cols"], "ldb_sc")
    mask_tok = ld(mask[:, :, :], d["mask"].rearrange("p (a m) -> p a m", a=8), "ldb_mask")
    spread_tok = ld(xn[:, 0, 0:P], d["spread"], "ldb_spread")
    wxdt_tok = ld(xn[0:NST, 1, :], d["wx"][2 * NST:NX, :], "ldb_wxdt")
    wdt_tok = ld(dx[0:NST, 0:NST], d["w_dtT"], "ldb_wdt")
    tok = Q.put("dve", lambda e: e.tensor_copy(spread[:, :], xn[:, 0, 0:P]), [spread_tok], "setb_dve")
    for ap in (halo[:, :, :, :], zeros[:, :], g[:, 3, :]):
        tok = Q.put("dve", lambda e, ap=ap: e.memset(ap, 0.0), (), "setb_dve")
    ones_tok = Q.put("dve", lambda e: e.memset(sg[:, 0:P], 1.0), (), "setb_dve")
    for ct in range(CT):
        tok = Q.put("pe", lambda e, ct=ct: e.matmul(
            misc[0][:, ct * NST:(ct + 1) * NST], xn[0:NST, 1, ct * P:(ct + 1) * P], dx[0:NST, 0:NST],
            start=True, stop=True), [wxdt_tok, wdt_tok], "setb_pe" if ct == CT - 1 else None)
    tok = Q.put("act", lambda e: e.activation(
        wx[:, :, 2 * NST:NX], misc[0][:, 0:CT * NST].rearrange("p (t k) -> p t k", t=CT), ACT.Copy),
        [tok], "setb_act")
    misc_free[0] = tok
    tmp = ygT
    for ct in range(CT):
        tok = Q.put("dve", lambda e, ct=ct: e.tensor_scalar(
            tmp[:, ct, 0:NX], wx[:, ct, :], cols[:, 1, ct:ct + 1], None, ALU.mult),
            [tok, wx_tok, cols_tok[1], cols_tok[0]], "setb_dve")
    for ct in range(CT):
        tok = Q.put("dve", lambda e, ct=ct: e.tensor_scalar(
            wx[:, ct, :], wx[:, ct, :], cols[:, 0, ct:ct + 1], None, ALU.mult), [tok], "setb_dve")
    for n, (src, dst) in enumerate(((wx, gw), (tmp, bw))):
        for ct in range(CT):
            mm = Q.put("pe", lambda e, ct=ct, n=n, src=src: e.matmul(
                misc[n][:, 0:NX], sg[:, 0:P], src[:, ct, 0:NX], start=ct == 0, stop=ct == CT - 1),
                [tok, misc_free[n], ones_tok], "setb_pe" if ct == CT - 1 else None)
        misc_free[n] = Q.put("act", lambda e, n=n, dst=dst: e.activation(dst[:, :], misc[n][:, 0:NX], ACT.Copy),
                             [mm], "setb_act")
    tok = Q.put("act", lambda e: e.activation(a_neg[:, :], state_cols[:, 1:2], ACT.Tanh), [sc_tok], "setb_act")
    set_tok = Q.put("dve", lambda e: e.tensor_scalar(a_neg[:, :], a_neg[:, :], -1.0, None, ALU.mult),
                    [tok], "setb_dve")
    for e in Q.q:
        for tk in [w_in_tok, w_out_tok, wconv_tok, temb_tok, sc_tok, mask_tok, set_tok] + aff_tok + cols_tok:
            Q.wait(e, tk)
    barrier(Q, "b2")

    F = {}
    par_ready = [None, None]
    xhl_tok = {}
    cexp_free, cexp_ready = [None, None], [None, None]
    scan_free = [None, None]
    last_decay = [None]
    cd_tok = {}

    x2T_tok = [None]

    def load_x2T(i, hb):
        for it in range(HT):
            x2T_tok[0] = Q.dma(x2T[:, it, :, :],
                               d["x2T"][it * P:(it + 1) * P, hb * HB:(hb + 1) * HB, i * TOK:(i + 1) * TOK],
                               [F.get("x2T")], "ldb_x2T")

    def prepare(i, banks):
        t0, par_i = i * TOK, i % 2
        for hb in range(2):
            b0 = hb * HB
            if not (i or hb):
                load_x2T(0, 0)
            x_tok = x2T_tok[0]

            def xr_tile(ct, it, m):
                return Q.put("pe", lambda e: e.matmul(
                    misc[m][:, :], w_in[:, it, ct * P:(ct + 1) * P],
                    x2T[:, it, :, :].rearrange("p b q -> p (b q)"), start=it == 0, stop=it == HT - 1),
                    [x_tok, misc_free[m]], "xr_pe" if it == HT - 1 else None)

            def xr_out(ct, m, mm, b0=b0):
                k = ct % 2
                hl = Q.put("act", lambda e: e.activation(
                    xr[:, k, :, 0:TAPS - 1], halo[:, ct, b0:b0 + HB, :], ACT.Copy), [F.get(("xr", k))], "xr_act")
                for bb in range(HB):
                    ev = Q.put("act", lambda e, bb=bb: e.activation(
                        xr[:, k, bb, TAPS - 1:], misc[m][:, bb * TOK:(bb + 1) * TOK], ACT.Identity,
                        bias=temb[:, ct, b0 + bb:b0 + bb + 1]), [mm], "xr_act")
                misc_free[m] = ev
                tap = Q.put("act", lambda e: e.activation(
                    cv[:, k, :, :], xr[:, k, :, TAPS - 1:], ACT.Copy, scale=wconv[:, ct, TAPS - 1:TAPS]),
                    [ev, F.get(("cv", k))], "xr_act")
                halo_tok = Q.put("act", lambda e: e.activation(
                    halo[:, ct, b0:b0 + HB, :], xr[:, k, :, TOK:TOK + TAPS - 1], ACT.Copy), [hl], "xr_act")
                F[("xr", k)] = [halo_tok]
                return tap

            def conv_tap(ct, j, tap):
                k = ct % 2
                tap = Q.put("dve", lambda e: e.scalar_tensor_tensor(
                    cv[:, k, :, :], xr[:, k, :, j:j + TOK], wconv[:, ct, j:j + 1], cv[:, k, :, :],
                    ALU.mult, ALU.add), [tap], "conv_dve")
                if j == TAPS - 2:
                    F[("xr", k)].append(tap)
                return tap

            def silu(ct, tap):
                k = ct % 2
                F[("cv", k)] = Q.put("act", lambda e: e.activation(
                    xc[:, ct, :, :], cv[:, k, :, :], ACT.Silu, bias=cols[:, 2, ct:ct + 1]),
                    [tap, F.get("xc")], "silu_act")
                return F[("cv", k)]

            tap = None
            for ct in range(CT + 1):
                m = banks.take()
                for it in range(HT):
                    if ct < CT:
                        mm = xr_tile(ct, it, m)
                        yield MATMUL, MATMUL
                    else:
                        yield 0.0, 1.0
                    if ct > 0 and it > 0:
                        tap = conv_tap(ct - 1, it - 1, tap)
                before = tap
                if ct < CT:
                    tap = xr_out(ct, m, mm)
                if ct > 0:
                    xc_tok = silu(ct - 1, before)
                yield 0.0, 1.0
            F["x2T"] = mm
            if hb == 0 or i + 1 < NCH:
                load_x2T(i + hb, 1 - hb)

            def tokens_first(bb, half):
                m = banks.take()
                for c in range(4):
                    ct = half * 4 + c
                    tr = Q.put("pe", lambda e, c=c, ct=ct, m=m: e.transpose(
                        misc[m][:, c * P:(c + 1) * P], xc[:, ct, bb, :], ident[:, :]),
                        [xc_tok, misc_free[m]], "xc_pe" if c == 3 else None)
                return m, tr
            for bb in range(HB):
                for half in range(2):
                    m, tr = tokens_first(bb, half)
                    yield 0.5, 2.0
                    misc_free[m] = bn = Q.put("dve", lambda e, m=m, half=half, bb=bb: e.bn_stats(
                        st6[:, bb % 2, half, :], misc[m][:, :]), [tr], "bn_dve")
                    yield 0.0, 0.7
                ag = Q.put("dve", lambda e, bb=bb: e.bn_aggr(
                    mvb[:, bb, :], st6[:, bb % 2, :, :].rearrange("p a b -> p (a b)")), [bn], "bn_dve")
            tok = Q.put("dve", lambda e: e.tensor_scalar(rs[:, :], mvb[:, :, 1], EPS_LN, None, ALU.add),
                        [ag, F.get("rs")], "bn_dve")
            tok = Q.put("act", lambda e: e.activation(rs[:, :], rs[:, :], ACT.Sqrt), [tok], "bn_act")
            pending = None
            for bb in range(HB):
                m = banks.take()
                for ct in range(CT):
                    mm = Q.put("pe", lambda e, ct=ct, bb=bb, m=m: e.matmul(
                        misc[m][:, 0:NX], xc[:, ct, bb, :], wx[:, ct, :], start=ct == 0, stop=ct == CT - 1),
                        [xc_tok, misc_free[m]], "proj_pe" if ct == CT - 1 else None)
                    if ct % 4 == 3:
                        yield MATMUL, MATMUL
                yield 0.0, 1.5
                if bb == 0:
                    tok = Q.put("dve", lambda e: e.reciprocal(rs[:, :], rs[:, :]), [tok], "bn_dve")
                    nm_tok = Q.put("dve", lambda e: e.tensor_scalar(nm[:, :], mvb[:, :, 0], -1.0, None, ALU.mult),
                                   (), "bn_dve")
                    rs_tok = Q.put("dve", lambda e: e.tensor_tensor(nmr[:, :], nm[:, :], rs[:, :], ALU.mult),
                                   [tok, nm_tok], "bn_dve")
                three = lambda ap: ap.rearrange("p (k s) -> p k s", k=3)
                tok = Q.put("dve", lambda e, bb=bb, b0=b0, m=m: e.scalar_tensor_tensor(
                    proj[:, :, b0 + bb, :], three(gw[:, :]), nm[:, bb:bb + 1], three(misc[m][:, 0:NX]),
                    ALU.mult, ALU.add), [mm, rs_tok, F.get("proj")], "proj_dve")
                misc_free[m] = tok
                pr_tok = Q.put("dve", lambda e, bb=bb, b0=b0: e.scalar_tensor_tensor(
                    proj[:, :, b0 + bb, :], proj[:, :, b0 + bb, :], rs[:, bb:bb + 1], three(bw[:, :]),
                    ALU.mult, ALU.add), [tok], "proj_dve")
                yield 0.0, 0.5

            def xn_rows(bb):
                k = bb % 3
                for half in range(2):
                    m, tr = tokens_first(bb, half)
                    misc_free[m] = made[bb] = Q.put("act", lambda e, m=m, half=half: e.activation(
                        xn[:, k, half * BANK:(half + 1) * BANK], misc[m][:, :], ACT.Identity,
                        bias=nmr[:, bb:bb + 1], scale=rs[:, bb:bb + 1]), [tr, F.get(("xn", k))], "xn_act")
                    yield 0.5, 1.8

            def xn_affine(bb):
                k = bb % 3
                tok = Q.put("pool", lambda e: e.tensor_tensor(xn[:, k, :], xn[:, k, :], affine[:, 0, :],
                                                              ALU.mult), [made[bb]], "xn_pool")
                made[bb] = tok = Q.put("pool", lambda e: e.tensor_tensor(xn[:, k, :], xn[:, k, :], affine[:, 1, :],
                                                                         ALU.add), [tok], "xn_pool")
                return Q.put("pool", lambda e: e.tensor_tensor(dx[:, :], xn[:, k, :], affine[:, 2, :],
                                                               ALU.mult), [tok, F.get("dx")], "xn_pool")

            def xn_halves(bb, b):
                k = bb % 3
                hi = Q.put("act", lambda e: e.activation(xhi[:, bb % 2, :], xn[:, k, :], ACT.Copy),
                           [made[bb], F.get(("xhi", bb % 2))], "xn_act")
                made["squares"] = sqs = F["junk"] = Q.put("act", lambda e: e.activation(
                    junk[:, :], xn[:, k, :], ACT.Square, accum_out=sumsq[:, bb:bb + 1]),
                    [F.get("sumsq"), F.get("junk")], "xn_act")
                lo = Q.put("pool", lambda e: e.tensor_tensor(
                    xn[:, k, :].bitcast(F32R), xn[:, k, :], xhi[:, bb % 2, :].bitcast(F32), ALU.subtract),
                    [hi, sqs], "xn_pool")
                return hi, lo

            def store_halves(bb, b, hi, lo):
                k = bb % 3
                hi_st = Q.dma(d["xhl"][0, b, t0:t0 + TOK, :], xhi[:, bb % 2, :], [hi], f"st_xhi{bb % 2}")
                F[("xhi", bb % 2)] = [hi_st, lo]
                F[("xn", k)] = Q.dma(d["xhl"][1, b, t0:t0 + TOK, :], xn[:, k, :], [lo], f"st_xlo{k}")
                xhl_tok[i] = xhl_tok.get(i, []) + [hi_st, F[("xn", k)]]
            made, moments, dxt, halved = {}, {}, {}, {}
            for bb in range(HB + 1):
                if bb < HB:
                    yield from xn_rows(bb)
                if bb > 0:
                    yield 0.0, 0.0, 0.0, moments[bb - 1]
                    F["dx"] = Q.dma(d["dx"][b0 + bb - 1, t0:t0 + TOK, :], dx[:, :], [dxt[bb - 1]], "st_dx")
                if bb > 1:
                    store_halves(bb - 2, b0 + bb - 2, *halved[bb - 2])
                if bb < HB:
                    dxt[bb] = xn_affine(bb)
                    moments[bb] = yield 0.0, 0.2, 7.2
                if bb > 0:
                    halved[bb - 1] = xn_halves(bb - 1, b0 + bb - 1)
                    moments["lo"] = yield 0.0, 0.2, 2.4
            yield 0.0, 0.0, 0.0, moments["lo"]
            store_halves(HB - 1, b0 + HB - 1, *halved[HB - 1])
            F["xc"] = [("xc_pe", Q.count["xc_pe"]), ("proj_pe", Q.count["proj_pe"])]
            tok = Q.put("dve", lambda e: e.tensor_scalar(sumsq[:, :], sumsq[:, :], 1.0, None, ALU.min),
                        [made["squares"]], "norm2_dve")
            tok = Q.put("act", lambda e: e.activation(sumsq[:, :], sumsq[:, :], ACT.Sqrt), [tok], "bn_act")
            F["rs"] = [("xn_act", Q.count["xn_act"]), pr_tok]
            yield 0.0, 1.2
            for bb in range(HB):
                bt = Q.put("dve", lambda e, bb=bb, b0=b0: e.tensor_scalar(
                    proj[:, 0, b0 + bb, :], proj[:, 0, b0 + bb, :], sumsq[:, bb:bb + 1], None, ALU.mult),
                    [tok, pr_tok], "norm2_dve")
            F["sumsq"] = bt
            yield 0.0, 0.8
        m = banks.take()
        for k in range(3):
            tr = Q.put("pe", lambda e, k=k: e.transpose(
                misc[m][:, k * P:(k + 1) * P], proj[:, k, :, :].rearrange("p b s -> p (b s)"), ident[:, :]),
                [bt, misc_free[m]], "proj_pe" if k == 2 else None)
        F["proj"] = tr
        Q.put("act", lambda e: e.activation(
            par[:, 0:2, :], misc[m][:, 0:2 * P].rearrange("p (k q) -> p k q", k=2), ACT.Copy),
            [tr, F.get("par")], "par_act")
        misc_free[m] = th = Q.put("act", lambda e: e.activation(
            par[:, 2, :], misc[m][:, 2 * P:3 * P], ACT.Tanh, bias=state_cols[:, 0:1]), (), "par_act")
        yield 0.3, 5.0
        tok = Q.put("dve", lambda e: e.tensor_scalar(par[:, 2, :], par[:, 2, :], 0.01, a_neg[:, 0:1],
                                                     ALU.mult, ALU.mult), [th], "par_dve")
        tok = Q.put("dve", lambda e: e.tensor_scalar(par[:, 2, :], par[:, 2, :], 1.0, None, ALU.add),
                    [tok], "par_dve")
        init = 1.0 if i == 0 else decay[:, 1 - par_i, TOK - 1:TOK]
        dec = Q.put("dve", lambda e: e.tensor_tensor_scan(
            decay[:, par_i, :], par[:, 2, :], zeros[:, :], init, ALU.mult, ALU.add), [tok, last_decay[0]], "par_dve")
        last_decay[0] = dec
        yield 0.0, 1.2
        tok = Q.put("dve", lambda e: e.reciprocal(inv[:, :], decay[:, par_i, :]), [dec], "par_dve")
        Q.put("dve", lambda e: e.tensor_tensor(bd[:, par_i, :], par[:, 0, :], inv[:, :], ALU.mult),
              [tok, scan_free[par_i]], "par_dve")
        Q.put("dve", lambda e: e.tensor_scalar(lim[:, par_i, 0, :], inv[:, :], 10.0, None, ALU.mult), (), "par_dve")
        par_ready[par_i] = Q.put("dve", lambda e: e.tensor_scalar(
            lim[:, par_i, 1, :], inv[:, :], -10.0, None, ALU.mult), (), "par_dve")
        cd_tok[i] = F["par"] = Q.put("dve", lambda e: e.tensor_tensor(
            cd[:, par_i, :], par[:, 1, :], decay[:, par_i, :], ALU.mult), [dec], "par_dve")
        yield 0.0, 1.5
        yield from expand(i, 0)

    junk = sb("junk", [P, DIN], mybir.dt.bfloat16)

    def expand(i, h):
        A = HC // 8
        src = cd[:, i % 2, h * HC:(h + 1) * HC].rearrange("p (a j) -> p a j", j=8)
        for a in range(A):
            cexp_ready[h] = Q.put("pool", lambda e, a=a: e.tensor_tensor(
                cexp[:, h, a * 8:(a + 1) * 8, :], src[:, a, :].unsqueeze(2).broadcast_to([P, 8, 32]),
                mask[:, :, :], ALU.mult), [cd_tok[i], cexp_free[h]], "cexp_pool")
            yield 0.0, 0.8, 0.6

    sx_free, sx_tok = [None] * 2, {}
    xps_free, xps_ready = [None, None], {}
    ysb_free = [None, None]
    g_tok, g_free = {-1: None}, [None] * 4
    y_st = {}

    def load_unit(n):
        s, ts = n % 2, n * UNIT
        toks = xhl_tok[ts // TOK]
        for j in range(4):
            w = UNIT // 4
            sx_tok[n] = Q.dma(sx[32 * j:32 * j + 2 * B, s, :, :],
                              d["xhl"][:, :, ts + j * w:ts + (j + 1) * w, :].rearrange("h b t c -> (h b) t c"),
                              [toks, sx_free[s]], f"ld_sx{s}")

    def spread_x(tm):
        n, r = divmod(tm, UNIT)
        j, w = divmod(r, UNIT // 4)
        m = tm % 2
        for half in range(2):
            xps_ready[tm] = Q.put("pe", lambda e, half=half: e.matmul(
                xps[m][:, half * BANK:(half + 1) * BANK], spread[32 * j:32 * j + 2 * B, :],
                sx[32 * j:32 * j + 2 * B, n % 2, w, half * BANK:(half + 1) * BANK], start=True, stop=True),
                [sx_tok[n], xps_free[m]], "xps_pe" if half else None)
        if r == UNIT - 1:
            sx_free[n % 2] = xps_ready[tm]

    def step(tm):
        i, tl = divmod(tm, TOK)
        pi, s = i % 2, tm % 4
        q = Q.put("dve", lambda e: e.scalar_tensor_tensor(
            g[:, s, :], xps[tm % 2][:, :], bd[:, pi, tl:tl + 1], g[:, (tm - 1) % 4, :], ALU.mult, ALU.add),
            [xps_ready[tm], g_tok[tm - 1], par_ready[pi], g_free[s]], "scan_dve")
        xps_free[tm % 2] = q
        return q

    def clip(tm, q):
        i, tl = divmod(tm, TOK)
        pi, s = i % 2, tm % 4
        g_tok[tm] = Q.put("dve", lambda e: e.tensor_scalar(
            g[:, s, :], g[:, s, :], lim[:, pi, 0, tl:tl + 1], lim[:, pi, 1, tl:tl + 1], ALU.min, ALU.max),
            [q], "scan_dve")
        if tl == TOK - 1:
            scan_free[pi] = g_tok[tm]

    def outputs(tm):
        n, slot = tm // UNIT, tm % UNIT // 2
        m = n % 2
        for tp in range(2):
            h, tc = divmod((tm + tp) % TOK, HC)
            for half in range(2):
                j = 2 * tp + half
                tok = Q.put("pe", lambda e, tp=tp, half=half, j=j, h=h, tc=tc: e.matmul(
                    yps[m][32 * j:32 * (j + 1), :], cexp[:, h, tc, :],
                    g[:, (tm + tp) % 4, half * BANK:(half + 1) * BANK], start=slot == 0, stop=slot == 3),
                    [g_tok[tm + tp], cexp_ready[h], misc_free[2 + m]], "y_pe" if j == 3 else None)
        g_free[tm % 4] = g_free[(tm + 1) % 4] = tok
        cexp_free[h] = tok
        if slot == 3:
            misc_free[2 + m] = ev = Q.put("act", lambda e: e.activation(ysb[:, m, :], yps[m][:, :], ACT.Copy),
                                     [tok, ysb_free[m]], "y_act")
            for u in range(2):
                for half in range(2):
                    j = 2 * u + half
                    ysb_free[m] = Q.dma(
                        d["y"][:, n * UNIT:(n + 1) * UNIT, half * BANK:(half + 1) * BANK].rearrange(
                            "b (s u) c -> u s b c", u=2)[u], ysb[32 * j:32 * (j + 1), m, :], [ev], f"st_y{m}")
            y_st[n // (TOK // UNIT)] = [("st_y0", Q.count["st_y0"]), ("st_y1", Q.count.get("st_y1", 0))]

    room = {"y": y_t, "dx": dx_t, "sg": sg, "ygT": ygT, "x2": x2_t, "x2T": x2T_t}

    def finish(i, banks, room, batches, name=""):
        t0 = i * TOK
        y_t, dx_t, sg, ygT, x2_t, x2T_t = (room[k] for k in ("y", "dx", "sg", "ygT", "x2", "x2T"))
        R = last_read.setdefault(name, {})

        def load_gate(b):
            return Q.dma(x2T_t[:, :, :], d["x2T"][:, b, t0:t0 + TOK].rearrange("(t p) q -> p t q", p=P),
                         [R.get("x2T_t")], "ldf_x2T" + name)

        def leave(b, cp, x2_tok):
            m = banks.take()
            for ct in range(CT):
                mm = Q.put("pe", lambda e, ct=ct: e.matmul(
                    misc[m][:, :], ygT[:, ct, :], w_out[:, ct, :], start=ct == 0, stop=ct == CT - 1),
                    [cp, misc_free[m]], "out_pe" if ct == CT - 1 else None)
                yield MATMUL, MATMUL
            R["ygT"] = mm
            yield 0.0, 4.0
            misc_free[m] = tok = Q.put("dve", lambda e: e.tensor_tensor(
                x2_t[:, :], misc[m][:, :], x2_t[:, :], ALU.add), [mm, x2_tok], "out_dve")
            yield 0.0, 1.0
            R["x2_t"] = Q.dma(d["out"][b, t0:t0 + TOK, :], x2_t[:, :], [tok], "st_out" + name)
        for b in batches:
            if b == batches[0]:
                gx_tok = load_gate(b)
            dx_tok = Q.dma(dx_t[:, :], d["dx"][b, t0:t0 + TOK, :],
                           [("st_dx", dx_count[i]), R.get("dx_t")], "ldf_dx" + name)
            y_tok = Q.dma(y_t[:, :], d["y"][b, t0:t0 + TOK, :], [y_st[i], R.get("y_t")], "ldf_y" + name)
            yield 0.0, 3.0
            R["dx_t"] = tok = Q.put("pool", lambda e: e.tensor_tensor(y_t[:, :], y_t[:, :], dx_t[:, :], ALU.add),
                                    [y_tok, dx_tok], "yg_pool")
            yield 0.0, 0.2, 2.4
            for half in range(2):
                m = banks.take()
                for it in range(HT):
                    mm = Q.put("pe", lambda e, it=it, half=half, m=m: e.matmul(
                        misc[m][:, :], x2T_t[:, it, :], w_in[:, it, DIN + half * BANK:DIN + (half + 1) * BANK],
                        start=it == 0, stop=it == HT - 1), [gx_tok, misc_free[m]],
                        "gate_pe" if it == HT - 1 else None)
                    yield MATMUL, MATMUL
                misc_free[m] = sgt = Q.put("act", lambda e, half=half, m=m: e.activation(
                    sg[:, half * BANK:(half + 1) * BANK], misc[m][:, :], ACT.Silu), [mm, R.get("sg")], "gate_act")
                yield 0.0, 1.0
            R["x2T_t"] = mm
            if b != batches[-1]:
                gx_tok = load_gate(b + 1)
            tok = Q.put("pool", lambda e: e.tensor_tensor(y_t[:, :], y_t[:, :], sg[:, :], ALU.mult),
                        [tok, sgt], "yg_pool")
            R["sg"] = tok
            moment = yield 0.0, 0.2, 2.4
            if b != batches[0]:
                yield from leave(b - 1, cp, x2_tok)
            yield 0.0, 0.0, 0.0, moment
            for half in range(2):
                m = banks.take()
                for c in range(4):
                    ct = half * 4 + c
                    tr = Q.put("pe", lambda e, c=c, ct=ct, m=m: e.transpose(
                        misc[m][:, c * P:(c + 1) * P], y_t[:, ct * P:(ct + 1) * P], ident[:, :]),
                        [tok, misc_free[m]], "yg_pe" if c == 3 else None)
                misc_free[m] = cp = Q.put("act", lambda e, half=half, m=m: e.activation(
                    ygT[:, half * 4:(half + 1) * 4, :], misc[m][:, :].rearrange("p (t q) -> p t q", t=4),
                    ACT.Copy), [tr, R.get("ygT")], "yg_act")
                yield 0.5, 1.8
            R["y_t"] = tr
            x2_tok = Q.dma(x2_t[:, :], d["x2"][b, t0:t0 + TOK, :], [R.get("x2_t")], "ldf_x2" + name)
        yield from leave(batches[-1], cp, x2_tok)

    last_read = {}
    dx_count = {}
    for _ in prepare(0, Banks(0, 1, 2, 3)):
        pass
    dx_count[0] = Q.count["st_dx"]
    for n in range(2):
        load_unit(n)
    last_step = NCH * TOK
    spread_x(0)
    spread_x(1)
    lanes, fin = Lanes(), None
    for i in range(NCH):
        prep = [lanes.add(expand(i, 1))]
        if i + 1 < NCH:
            prep.append(lanes.add(prepare(i + 1, Banks(0)), after=prep[0]))
        if i > 0:
            fin = lanes.add(finish(i - 1, Banks(1), room, range(B)), after=fin)
        for tl in range(TOK):
            tm = i * TOK + tl
            work = SCAN_STEP - MATMUL + (-0.4 if tl % 2 else 0.5)
            q = step(tm)
            if tm + 2 < last_step:
                spread_x(tm + 2)
            lanes.advance(STEP / 2, work / 2)
            clip(tm, q)
            if tm % 2 == 1:
                outputs(tm - 1)
            nu = (tm + 2) // UNIT + 2
            if (tm + 2) % UNIT == UNIT - 1 and nu < last_step // UNIT:
                if nu * UNIT // TOK not in dx_count:
                    lanes.finish(prep, lambda: len(xhl_tok.get(i + 1, [])) == 2 * B)
                    dx_count[i + 1] = Q.count["st_dx"]
                load_unit(nu)
            lanes.advance(STEP / 2, work / 2)
        lanes.finish(prep)
    if fin:
        lanes.finish([fin])
    spare = {"y": xc[:, 0:2, :, :].rearrange("p a b q -> p (a b q)"),
             "dx": xc[:, 2:4, :, :].rearrange("p a b q -> p (a b q)"),
             "sg": xc[:, 4:6, :, :].rearrange("p a b q -> p (a b q)"),
             "ygT": xc[:, 6:8, :, :].rearrange("p a b q -> p (a b) q"), "x2": xn[:, 0, 0:HID],
             "x2T": x2T[:, :, 0, :]}
    last_read["B"] = {k: [F["x2T"], F[("xn", 0)], ("xn_act", Q.count["xn_act"])] + F["xc"]
                      for k in ("x2T_t", "dx_t", "x2_t", "y_t", "sg", "ygT")}
    lanes = [finish(NCH - 1, Banks(1, 3), room, range(0, HB)), finish(NCH - 1, Banks(0, 2), spare, range(HB, B), "B")]
    while lanes:
        lanes = [lane for lane in lanes if next(lane, None) is not None]
    for name in ("st_out", "st_outB"):
        Q.wait("sp", (name, Q.count[name]))
    ctx.close()


def program(nc, d, dims, only_attention=False):
    ctx = ExitStack()
    with ctx:
        Q = Queues(nc, ctx)
        sb = lambda n, s, dt=F32: ctx.enter_context(nc.sbuf_tensor(n, s, dt))
        t = {"ident": sb("ident", [P, P]), "ones32": sb("ones32", [P, 32])}
        ident, ones32 = t["ident"], t["ones32"]
        tok = Q.put("pool", lambda e: e.memset(ident[:, :], 0.0), signal="const_pool")
        Q.put("pool", lambda e: e.affine_select(out=ident[:, :], in_=ident[:, :], compare_op=ALU.not_equal, fill=1.0,
                                                base=0, pattern=[[-1, P]], channel_multiplier=1), [tok], "const_pool")
        tok = Q.put("pool", lambda e: e.memset(ones32[:, :], 1.0), signal="const_pool")
        Q.wait("pe", tok)
        attention_part(nc, Q, t, d, dims)
        if not only_attention:
            scan_part(nc, Q, t, d, dims)
        Q.emit()


_NAMES = ("x", "cond_2048", "L0_cond_q_weight", "L0_cond_k_weight", "L0_cond_v_weight", "L0_cond_w_weight",
          "L0_cond_u_weight", "L1_cond_W_in", "L1_cond_W_conv", "L1_cond_b_conv", "L1_cond_ln_g", "L1_cond_ln_b",
          "L1_cond_W_xproj", "L1_cond_W_dt", "L1_cond_b_dt", "L1_cond_A_log", "L1_cond_D", "L1_cond_W_out")


def kernel(**inputs):
    import concourse.bacc as bacc
    from concourse.bass_utils import run_bass_kernel_spmd

    nc = bacc.Bacc("TRN2", target_bir_lowering=False, num_devices=1)
    (x, cond, wq, wk, wv, ww, wu, w_in, w_conv, b_conv, ln_g, ln_b, w_x, w_dt, b_dt, a_log, dd, w_out) = (
        np.asarray(inputs[k]) for k in _NAMES)
    B, S = x.shape[:2]
    columns = lambda v: v.reshape(-1, P).T
    r, c = np.arange(P)[:, None], np.arange(P)[None, :]
    spread = ((r % 32 < 2 * B) & (r % 32 % B == c // NST)).astype(np.float32)
    j, m = np.arange(8)[None, :, None], np.arange(32)[None, None, :]
    mask = ((m // B == j // 2) & (m % B == r[:, :, None] // NST)).astype(np.float32).reshape(P, 8 * 32)
    given = {
        "x": x, "cond": cond, "condT": cond.T, "wqT": wq.T, "wkT": wk.T, "wvT": wv.T, "wwT": ww.T, "wuT": wu.T,
        "w_inT": w_in.T, "w_conv": w_conv.reshape(DIN, -1), "b_conv_cols": columns(b_conv), "ln_g": ln_g,
        "ln_b": ln_b, "ln_g_cols": columns(ln_g), "ln_b_cols": columns(ln_b), "wx": w_x, "wxT": w_x.T,
        "w_dtT": w_dt.T, "state_cols": np.stack([np.tile(b_dt, B), np.tile(a_log, B)], axis=1), "D": dd,
        "w_outT": w_out.T, "spread": spread, "mask": mask,
    }
    arrays, d = {}, {}
    for name, a in given.items():
        a = np.ascontiguousarray(a)
        arrays[f"in_{name}"] = a
        d[name] = nc.dram_tensor(f"in_{name}", a.shape, mybir.dt.from_np(a.dtype), kind="ExternalInput").ap()
    for name, shape, dt in (("rows", (B, 3, HID), F32), ("xs", (B, S, HID), F32), ("x2", (B, S, HID), F32), ("x2T", (HID, B, S), F32),
                            ("dx", (B, S, DIN), F32), ("xhl", (2, B, S, DIN), F32R),
                            ("y", (B, S, DIN), F32)):
        d[name] = nc.dram_tensor(f"scratch_{name}", shape, dt, kind="Internal").ap()
    d["out"] = nc.dram_tensor("out", (B, S, HID), F32, kind="ExternalOutput").ap()
    program(nc, d, {"B": B, "S": S})
    return run_bass_kernel_spmd(nc, [arrays], core_ids=[0]).results[0]["out"]
```
